# Optimizing a Trainium2 kernel written in Bass

```python
import numpy as np
import jax
import jax.numpy as jnp

def _softmax(x, axis=-1):
    return jax.nn.softmax(x, axis=axis)
def _gelu(x):
    return jax.nn.gelu(x, approximate=True)
def _silu(x):
    return jax.nn.silu(x)
def _sigmoid(x):
    return jax.nn.sigmoid(x)
def _layernorm(x, axis=-1, eps=1e-5):
    m = jnp.mean(x, axis=axis, keepdims=True)
    v = jnp.var(x, axis=axis, keepdims=True)
    return (x - m) / jnp.sqrt(v + eps)
def _scatter_add(tgt, idx, src, axis=0):
    return tgt.at[idx].add(src)
def _segment_sum(src, seg, n):
    return jax.ops.segment_sum(src, seg, n)

kernel_name = 'mk_metaformer_d2_conv_nchw384_1a81e6'

def setup_inputs(seed: int = 0):
    np.random.seed(seed)
    _w = jnp.asarray
    def _rec_inputs():
        import jax
        import jax.numpy as jnp
        _gk = jax.random.key(seed)
        x = -0.001003 + 1 * jax.random.normal(jax.random.fold_in(_gk, 1), (4, 384, 32, 32), jnp.float32)
        return x
    x = _rec_inputs()
    def _L0_conv_setup():
        import jax, jax.numpy as jnp
        import numpy as np
        D_MODEL = 192
        D_STATE = 16
        SSM_RATIO = 2.0
        D_INNER = int(SSM_RATIO * D_MODEL)
        DT_RANK = int(np.ceil(D_MODEL / 16))
        K_GROUP = 4
        BATCH, HH, WW = (4, 32, 32)
        DT_MIN, DT_MAX = (0.001, 0.1)
        LN_EPS = 1e-05

        def _cross_scan(x):
            B, D, H, W = x.shape
            x0 = x.reshape(B, D, H * W)
            x1 = jnp.transpose(x, (0, 1, 3, 2)).reshape(B, D, H * W)
            return jnp.stack([x0, x1, x0[..., ::-1], x1[..., ::-1]], axis=1)

        def _cross_merge(ys, H, W):
            B, K, D, L = ys.shape
            y0 = ys[:, 0]
            y2 = ys[:, 2][..., ::-1]
            yt = ys[:, 1] + ys[:, 3][..., ::-1]
            yt = jnp.transpose(yt.reshape(B, D, W, H), (0, 1, 3, 2)).reshape(B, D, L)
            return y0 + y2 + yt

        def _selective_scan(u, dt, A, Bs, Cs):
            dt_l = jnp.moveaxis(dt, -1, 0)
            u_l = jnp.moveaxis(u, -1, 0)
            B_l = jnp.moveaxis(Bs, -1, 0)
            C_l = jnpp_move = jnp.moveaxis(Cs, -1, 0)

            def step(h, inp):
                dtt, ut, bt, ct = inp
                dA = jnp.exp(dtt[..., None] * A)
                h = h * dA + (dtt * ut)[..., None] * bt[:, :, None, :]
                y = jnp.einsum('bkdn,bkn->bkd', h, ct)
                return (h, y)
            h0 = jnp.zeros(u.shape[:3] + (A.shape[-1],), dtype=u.dtype)
            _, ys = jax.lax.scan(step, h0, (dt_l, u_l, B_l, C_l))
            return jnp.moveaxis(ys, 0, -1)
        key = jax.random.key(seed)
        ks = jax.random.split(key, 6)
        x = jax.random.normal(ks[0], (BATCH, D_INNER, HH, WW), dtype=jnp.float32)
        x_proj_weight = jax.random.normal(ks[1], (K_GROUP, DT_RANK + 2 * D_STATE, D_INNER), dtype=jnp.float32) * D_INNER ** (-0.5)
        dt_projs_weight = jax.random.normal(ks[2], (K_GROUP, D_INNER, DT_RANK), dtype=jnp.float32) * DT_RANK ** (-0.5)
        dt = jnp.exp(jax.random.uniform(ks[3], (K_GROUP, D_INNER)) * (np.log(DT_MAX) - np.log(DT_MIN)) + np.log(DT_MIN))
        dt = jnp.clip(dt, 0.0001, None)
        dt_projs_bias = dt + jnp.log(-jnp.expm1(-dt))
        A = jnp.tile(jnp.arange(1, D_STATE + 1, dtype=jnp.float32)[None, :], (K_GROUP * D_INNER, 1))
        A_logs = jnp.log(A)
        Ds = jnp.ones((K_GROUP * D_INNER,), dtype=jnp.float32)
        ln_weight = jnp.ones((D_INNER,), dtype=jnp.float32)
        ln_bias = jnp.zeros((D_INNER,), dtype=jnp.float32)
        return {'x': x, 'x_proj_weight': x_proj_weight, 'dt_projs_weight': dt_projs_weight, 'dt_projs_bias': dt_projs_bias, 'A_logs': A_logs, 'Ds': Ds, 'ln_weight': ln_weight, 'ln_bias': ln_bias}
    _L0_conv_all = _L0_conv_setup()
    _L0_conv_in = {k: v for k, v in _L0_conv_all.items() if k in ('x_proj_weight', 'dt_projs_weight', 'dt_projs_bias', 'A_logs', 'Ds', 'ln_weight', 'ln_bias', )}
    del _L0_conv_all

    def _L0_ffn_setup():
        import jax, jax.numpy as jnp
        import numpy as np
        D_MODEL = 384
        D_FF = 1536
        key = jax.random.key(seed)
        k_x, k1, k2, k3, k4 = jax.random.split(key, 5)
        std = 0.02
        return {'x': jax.random.normal(k_x, (16, 2048, D_MODEL), dtype=jnp.float32), 'c_fc_1': std * jax.random.normal(k1, (1536, 32), dtype=jnp.float32), 'c_fc_2': std * jax.random.normal(k2, (1, 12), dtype=jnp.float32), 'c_proj_1': std * jax.random.normal(k3, (32, 1536), dtype=jnp.float32), 'c_proj_2': std * jax.random.normal(k4, (12, 1), dtype=jnp.float32)}
    _L0_ffn_all = _L0_ffn_setup()
    _L0_ffn_in = {k: v for k, v in _L0_ffn_all.items() if k in ('c_fc_1', 'c_fc_2', 'c_proj_1', 'c_proj_2', )}
    del _L0_ffn_all

    def _L1_conv_setup():
        import jax, jax.numpy as jnp
        import numpy as np
        D_MODEL = 384
        D_STATE = 16
        D_CONV = 4
        D_INNER = 2 * D_MODEL
        DT_RANK = -(-D_MODEL // 16)
        B_SZ, H_SZ, W_SZ = (4, 48, 48)
        LN_EPS = 1e-05

        def _mamba_block(x, in_proj_w, conv_w, conv_b, x_proj_w, dt_proj_w, dt_proj_b, A_log, D, out_proj_w, ln_gamma, ln_beta):
            b, c, h, w = x.shape
            L = h * w
            xs = x.transpose(0, 2, 3, 1).reshape(b, L, c)
            xz = xs @ in_proj_w.T
            xin, z = jnp.split(xz, 2, axis=-1)
            xc = jnp.pad(xin.transpose(0, 2, 1), ((0, 0), (0, 0), (D_CONV - 1, 0)))
            xc = jax.lax.conv_general_dilated(xc, conv_w[:, None, :], (1,), 'VALID', dimension_numbers=('NCH', 'OIH', 'NCH'), feature_group_count=D_INNER)
            xin = jax.nn.silu((xc + conv_b[None, :, None]).transpose(0, 2, 1))
            x_dbl = xin @ x_proj_w.T
            dt, Bm, Cm = jnp.split(x_dbl, [DT_RANK, DT_RANK + D_STATE], axis=-1)
            dt = jax.nn.softplus(dt @ dt_proj_w.T + dt_proj_b)
            A = -jnp.exp(A_log)

            def step(h_prev, inp):
                x_t, dt_t, B_t, C_t = inp
                dA = jnp.exp(dt_t[..., None] * A)
                dBx = dt_t[..., None] * B_t[:, None, :] * x_t[..., None]
                h_new = dA * h_prev + dBx
                y_t = jnp.einsum('bds,bs->bd', h_new, C_t)
                return (h_new, y_t)
            h0 = jnp.zeros((b, D_INNER, D_STATE), xin.dtype)
            seq = (xin.transpose(1, 0, 2), dt.transpose(1, 0, 2), Bm.transpose(1, 0, 2), Cm.transpose(1, 0, 2))
            _, ys = jax.lax.scan(step, h0, seq)
            y = ys.transpose(1, 0, 2) + xin * D
            y = y * jax.nn.silu(z)
            out = y @ out_proj_w.T
            mu = out.mean(-1, keepdims=True)
            var = out.var(-1, keepdims=True)
            out = (out - mu) * jax.lax.rsqrt(var + LN_EPS) * ln_gamma + ln_beta
            return out.reshape(b, h, w, c).transpose(0, 3, 1, 2)
        key = jax.random.key(seed)
        ks = jax.random.split(key, 8)
        sc = lambda k, shape, s: jax.random.normal(k, shape, jnp.float32) * s
        x = jax.random.normal(ks[0], (B_SZ, D_MODEL, H_SZ, W_SZ), jnp.float32)
        in_proj_w = sc(ks[1], (2 * D_INNER, D_MODEL), D_MODEL ** (-0.5))
        conv_w = sc(ks[2], (D_INNER, D_CONV), D_CONV ** (-0.5))
        conv_b = jnp.zeros((D_INNER,), jnp.float32)
        x_proj_w = sc(ks[3], (DT_RANK + 2 * D_STATE, D_INNER), D_INNER ** (-0.5))
        dt_proj_w = sc(ks[4], (D_INNER, DT_RANK), DT_RANK ** (-0.5))
        dt_proj_b = jnp.full((D_INNER,), jnp.log(jnp.expm1(0.01)), jnp.float32)
        A_log = jnp.log(jnp.tile(jnp.arange(1, D_STATE + 1, dtype=jnp.float32), (D_INNER, 1)))
        D = jnp.ones((D_INNER,), jnp.float32)
        out_proj_w = sc(ks[5], (D_MODEL, D_INNER), D_INNER ** (-0.5))
        ln_gamma = jnp.ones((D_MODEL,), jnp.float32)
        ln_beta = jnp.zeros((D_MODEL,), jnp.float32)
        return {'x': x, 'in_proj_w': in_proj_w, 'conv_w': conv_w, 'conv_b': conv_b, 'x_proj_w': x_proj_w, 'dt_proj_w': dt_proj_w, 'dt_proj_b': dt_proj_b, 'A_log': A_log, 'D': D, 'out_proj_w': out_proj_w, 'ln_gamma': ln_gamma, 'ln_beta': ln_beta}
    _L1_conv_all = _L1_conv_setup()
    _L1_conv_in = {k: v for k, v in _L1_conv_all.items() if k in ('in_proj_w', 'conv_w', 'conv_b', 'x_proj_w', 'dt_proj_w', 'dt_proj_b', 'A_log', 'D', 'out_proj_w', 'ln_gamma', 'ln_beta', )}
    del _L1_conv_all

    def _L1_ffn_setup():
        import jax, jax.numpy as jnp
        import numpy as np
        NUM_EXPERTS = 4
        TOP_K = 2
        DIM = 384
        HID = 4 * DIM
        key = jax.random.key(seed)
        ks = jax.random.split(key, 5)
        B, S = (16, 2048)
        scale_in = 1.0 / np.sqrt(DIM)
        scale_hid = 1.0 / np.sqrt(HID)
        return {'x': jax.random.normal(ks[0], (B, S, DIM), dtype=jnp.float32), 'gate_w': jax.random.normal(ks[1], (DIM, NUM_EXPERTS), dtype=jnp.float32) * scale_in, 'gate_b': jnp.zeros((NUM_EXPERTS,), dtype=jnp.float32), 'w1': jax.random.normal(ks[2], (NUM_EXPERTS, DIM, HID), dtype=jnp.float32) * scale_in, 'b1': jnp.zeros((NUM_EXPERTS, HID), dtype=jnp.float32), 'w2': jax.random.normal(ks[3], (NUM_EXPERTS, HID, DIM), dtype=jnp.float32) * scale_hid, 'b2': jnp.zeros((NUM_EXPERTS, DIM), dtype=jnp.float32)}
    _L1_ffn_all = _L1_ffn_setup()
    _L1_ffn_in = {k: v for k, v in _L1_ffn_all.items() if k in ('gate_w', 'gate_b', 'w1', 'b1', 'w2', 'b2', )}
    del _L1_ffn_all

    return {
        "x": x,
        "L0_conv_x_proj_weight": _L0_conv_in["x_proj_weight"],
        "L0_conv_dt_projs_weight": _L0_conv_in["dt_projs_weight"],
        "L0_conv_dt_projs_bias": _L0_conv_in["dt_projs_bias"],
        "L0_conv_A_logs": _L0_conv_in["A_logs"],
        "L0_conv_Ds": _L0_conv_in["Ds"],
        "L0_conv_ln_weight": _L0_conv_in["ln_weight"],
        "L0_conv_ln_bias": _L0_conv_in["ln_bias"],
        "L0_ffn_c_fc_1": _L0_ffn_in["c_fc_1"],
        "L0_ffn_c_fc_2": _L0_ffn_in["c_fc_2"],
        "L0_ffn_c_proj_1": _L0_ffn_in["c_proj_1"],
        "L0_ffn_c_proj_2": _L0_ffn_in["c_proj_2"],
        "L1_conv_in_proj_w": _L1_conv_in["in_proj_w"],
        "L1_conv_conv_w": _L1_conv_in["conv_w"],
        "L1_conv_conv_b": _L1_conv_in["conv_b"],
        "L1_conv_x_proj_w": _L1_conv_in["x_proj_w"],
        "L1_conv_dt_proj_w": _L1_conv_in["dt_proj_w"],
        "L1_conv_dt_proj_b": _L1_conv_in["dt_proj_b"],
        "L1_conv_A_log": _L1_conv_in["A_log"],
        "L1_conv_D": _L1_conv_in["D"],
        "L1_conv_out_proj_w": _L1_conv_in["out_proj_w"],
        "L1_conv_ln_gamma": _L1_conv_in["ln_gamma"],
        "L1_conv_ln_beta": _L1_conv_in["ln_beta"],
        "L1_ffn_gate_w": _L1_ffn_in["gate_w"],
        "L1_ffn_gate_b": _L1_ffn_in["gate_b"],
        "L1_ffn_w1": _L1_ffn_in["w1"],
        "L1_ffn_b1": _L1_ffn_in["b1"],
        "L1_ffn_w2": _L1_ffn_in["w2"],
        "L1_ffn_b2": _L1_ffn_in["b2"],
    }

def reference(x, L0_conv_x_proj_weight, L0_conv_dt_projs_weight, L0_conv_dt_projs_bias, L0_conv_A_logs, L0_conv_Ds, L0_conv_ln_weight, L0_conv_ln_bias, L0_ffn_c_fc_1, L0_ffn_c_fc_2, L0_ffn_c_proj_1, L0_ffn_c_proj_2, L1_conv_in_proj_w, L1_conv_conv_w, L1_conv_conv_b, L1_conv_x_proj_w, L1_conv_dt_proj_w, L1_conv_dt_proj_b, L1_conv_A_log, L1_conv_D, L1_conv_out_proj_w, L1_conv_ln_gamma, L1_conv_ln_beta, L1_ffn_gate_w, L1_ffn_gate_b, L1_ffn_w1, L1_ffn_b1, L1_ffn_w2, L1_ffn_b2):
    import jax
    import jax.numpy as jnp
    def _L0_conv_ref(x, x_proj_weight, dt_projs_weight, dt_projs_bias, A_logs, Ds, ln_weight, ln_bias):
        import jax, jax.numpy as jnp
        import numpy as np
        D_MODEL = 192
        D_STATE = 16
        SSM_RATIO = 2.0
        D_INNER = int(SSM_RATIO * D_MODEL)
        DT_RANK = int(np.ceil(D_MODEL / 16))
        K_GROUP = 4
        BATCH, HH, WW = (4, 32, 32)
        DT_MIN, DT_MAX = (0.001, 0.1)
        LN_EPS = 1e-05

        def _cross_scan(x):
            B, D, H, W = x.shape
            x0 = x.reshape(B, D, H * W)
            x1 = jnp.transpose(x, (0, 1, 3, 2)).reshape(B, D, H * W)
            return jnp.stack([x0, x1, x0[..., ::-1], x1[..., ::-1]], axis=1)

        def _cross_merge(ys, H, W):
            B, K, D, L = ys.shape
            y0 = ys[:, 0]
            y2 = ys[:, 2][..., ::-1]
            yt = ys[:, 1] + ys[:, 3][..., ::-1]
            yt = jnp.transpose(yt.reshape(B, D, W, H), (0, 1, 3, 2)).reshape(B, D, L)
            return y0 + y2 + yt

        def _selective_scan(u, dt, A, Bs, Cs):
            dt_l = jnp.moveaxis(dt, -1, 0)
            u_l = jnp.moveaxis(u, -1, 0)
            B_l = jnp.moveaxis(Bs, -1, 0)
            C_l = jnpp_move = jnp.moveaxis(Cs, -1, 0)

            def step(h, inp):
                dtt, ut, bt, ct = inp
                dA = jnp.exp(dtt[..., None] * A)
                h = h * dA + (dtt * ut)[..., None] * bt[:, :, None, :]
                y = jnp.einsum('bkdn,bkn->bkd', h, ct)
                return (h, y)
            h0 = jnp.zeros(u.shape[:3] + (A.shape[-1],), dtype=u.dtype)
            _, ys = jax.lax.scan(step, h0, (dt_l, u_l, B_l, C_l))
            return jnp.moveaxis(ys, 0, -1)
        B, D, H, W = x.shape
        K = x_proj_weight.shape[0]
        N = D_STATE
        R = dt_projs_weight.shape[-1]
        L = H * W
        xs = _cross_scan(x)
        x_dbl = jnp.einsum('bkdl,kcd->bkcl', xs, x_proj_weight)
        dts, Bs, Cs = (x_dbl[:, :, :R], x_dbl[:, :, R:R + N], x_dbl[:, :, R + N:])
        dts = jnp.einsum('bkrl,kdr->bkdl', dts, dt_projs_weight)
        A = -jnp.exp(A_logs.astype(jnp.float32)).reshape(K, D, N)
        dt = jax.nn.softplus(dts.astype(jnp.float32) + dt_projs_bias.astype(jnp.float32)[None, :, :, None])
        u = xs.astype(jnp.float32)
        Bs = Bs.astype(jnp.float32)
        Cs = Cs.astype(jnp.float32)
        ys = _selective_scan(u, dt, A, Bs, Cs)
        ys = ys + Ds.astype(jnp.float32).reshape(K, D)[None, :, :, None] * u
        y = _cross_merge(ys, H, W).reshape(B, D, H, W)
        yc = jnp.transpose(y, (0, 2, 3, 1))
        mu = jnp.mean(yc, axis=-1, keepdims=True)
        var = jnp.mean((yc - mu) ** 2, axis=-1, keepdims=True)
        yc = (yc - mu) * jax.lax.rsqrt(var + LN_EPS) * ln_weight + ln_bias
        y = jnp.transpose(yc, (0, 3, 1, 2)).astype(x.dtype)
        return jax.nn.gelu(y, approximate=False)

    def _L0_ffn_ref(x, c_fc_1, c_fc_2, c_proj_1, c_proj_2):
        import jax, jax.numpy as jnp
        import numpy as np
        D_MODEL = 384
        D_FF = 1536
        w_fc = jnp.kron(c_fc_1, c_fc_2)
        w_proj = jnp.kron(c_proj_1, c_proj_2)
        h = x @ w_fc.T
        h = jax.nn.gelu(h, approximate=False)
        out = h @ w_proj.T
        return out

    def _L1_conv_ref(x, in_proj_w, conv_w, conv_b, x_proj_w, dt_proj_w, dt_proj_b, A_log, D, out_proj_w, ln_gamma, ln_beta):
        import jax, jax.numpy as jnp
        import numpy as np
        D_MODEL = 384
        D_STATE = 16
        D_CONV = 4
        D_INNER = 2 * D_MODEL
        DT_RANK = -(-D_MODEL // 16)
        B_SZ, H_SZ, W_SZ = (4, 48, 48)
        LN_EPS = 1e-05

        def _mamba_block(x, in_proj_w, conv_w, conv_b, x_proj_w, dt_proj_w, dt_proj_b, A_log, D, out_proj_w, ln_gamma, ln_beta):
            b, c, h, w = x.shape
            L = h * w
            xs = x.transpose(0, 2, 3, 1).reshape(b, L, c)
            xz = xs @ in_proj_w.T
            xin, z = jnp.split(xz, 2, axis=-1)
            xc = jnp.pad(xin.transpose(0, 2, 1), ((0, 0), (0, 0), (D_CONV - 1, 0)))
            xc = jax.lax.conv_general_dilated(xc, conv_w[:, None, :], (1,), 'VALID', dimension_numbers=('NCH', 'OIH', 'NCH'), feature_group_count=D_INNER)
            xin = jax.nn.silu((xc + conv_b[None, :, None]).transpose(0, 2, 1))
            x_dbl = xin @ x_proj_w.T
            dt, Bm, Cm = jnp.split(x_dbl, [DT_RANK, DT_RANK + D_STATE], axis=-1)
            dt = jax.nn.softplus(dt @ dt_proj_w.T + dt_proj_b)
            A = -jnp.exp(A_log)

            def step(h_prev, inp):
                x_t, dt_t, B_t, C_t = inp
                dA = jnp.exp(dt_t[..., None] * A)
                dBx = dt_t[..., None] * B_t[:, None, :] * x_t[..., None]
                h_new = dA * h_prev + dBx
                y_t = jnp.einsum('bds,bs->bd', h_new, C_t)
                return (h_new, y_t)
            h0 = jnp.zeros((b, D_INNER, D_STATE), xin.dtype)
            seq = (xin.transpose(1, 0, 2), dt.transpose(1, 0, 2), Bm.transpose(1, 0, 2), Cm.transpose(1, 0, 2))
            _, ys = jax.lax.scan(step, h0, seq)
            y = ys.transpose(1, 0, 2) + xin * D
            y = y * jax.nn.silu(z)
            out = y @ out_proj_w.T
            mu = out.mean(-1, keepdims=True)
            var = out.var(-1, keepdims=True)
            out = (out - mu) * jax.lax.rsqrt(var + LN_EPS) * ln_gamma + ln_beta
            return out.reshape(b, h, w, c).transpose(0, 3, 1, 2)
        return _mamba_block(x, in_proj_w, conv_w, conv_b, x_proj_w, dt_proj_w, dt_proj_b, A_log, D, out_proj_w, ln_gamma, ln_beta)

    def _L1_ffn_ref(x, gate_w, gate_b, w1, b1, w2, b2):
        import jax, jax.numpy as jnp
        import numpy as np
        NUM_EXPERTS = 4
        TOP_K = 2
        DIM = 384
        HID = 4 * DIM
        scores = jnp.einsum('bsd,de->bse', x, gate_w) + gate_b
        probs = jax.nn.softmax(scores, axis=-1)
        topk_vals, topk_idx = jax.lax.top_k(probs, TOP_K)
        mask = jnp.sum(jax.nn.one_hot(topk_idx, NUM_EXPERTS, dtype=probs.dtype), axis=-2)
        masked = probs * mask
        masked = masked / (jnp.sum(masked, axis=-1, keepdims=True) + 1e-09)
        h = jax.nn.gelu(jnp.einsum('bsd,edh->ebsh', x, w1) + b1[:, None, None, :], approximate=False)
        y = jnp.einsum('ebsh,ehd->ebsd', h, w2) + b2[:, None, None, :]
        out = jnp.einsum('bse,ebsd->bsd', masked, y)
        return out

    def _gn(v, G=32, eps=1e-5):
        B_, C_, H_, W_ = v.shape
        g = v.reshape(B_, G, C_ // G, H_, W_)
        m = jnp.mean(g, axis=(2, 3, 4), keepdims=True)
        s = jnp.var(g, axis=(2, 3, 4), keepdims=True)
        return ((g - m) / jnp.sqrt(s + eps)).reshape(v.shape)

    def _ln_c(v, eps=1e-6):
        m = jnp.mean(v, axis=1, keepdims=True)
        s = jnp.var(v, axis=1, keepdims=True)
        return (v - m) / jnp.sqrt(s + eps)

    def _ln_t(v, eps=1e-5):
        m = jnp.mean(v, axis=-1, keepdims=True)
        s = jnp.var(v, axis=-1, keepdims=True)
        return (v - m) / jnp.sqrt(s + eps)

    def _to_tokens(v):
        B_, C_, H_, W_ = v.shape
        return v.reshape(B_, C_, H_ * W_).transpose(0, 2, 1)
    def _from_tokens(t, like):
        B_, C_, H_, W_ = like.shape
        return t.transpose(0, 2, 1).reshape(B_, C_, H_, W_)

    x = x + _L0_conv_ref(_ln_c(x), L0_conv_x_proj_weight, L0_conv_dt_projs_weight, L0_conv_dt_projs_bias, L0_conv_A_logs, L0_conv_Ds, L0_conv_ln_weight, L0_conv_ln_bias)
    t = _to_tokens(x)
    t = t + _L0_ffn_ref(_ln_t(t), L0_ffn_c_fc_1, L0_ffn_c_fc_2, L0_ffn_c_proj_1, L0_ffn_c_proj_2)
    x = _from_tokens(t, x)
    x = x + _L1_conv_ref(_ln_c(x), L1_conv_in_proj_w, L1_conv_conv_w, L1_conv_conv_b, L1_conv_x_proj_w, L1_conv_dt_proj_w, L1_conv_dt_proj_b, L1_conv_A_log, L1_conv_D, L1_conv_out_proj_w, L1_conv_ln_gamma, L1_conv_ln_beta)
    t = _to_tokens(x)
    t = t + _L1_ffn_ref(_ln_t(t), L1_ffn_gate_w, L1_ffn_gate_b, L1_ffn_w1, L1_ffn_b1, L1_ffn_w2, L1_ffn_b2)
    x = _from_tokens(t, x)
    return x


_drawn_inputs = setup_inputs


def setup_inputs(seed=0):
    import zlib

    import numpy as np

    out = dict(_drawn_inputs(seed))
    spreads = {'L0_conv_Ds': (1.0, 0.2),
     'L0_conv_ln_weight': (1.0, 0.2),
     'L0_conv_ln_bias': (0.0, 0.1),
     'L1_conv_conv_b': (0.0, 0.1),
     'L1_conv_dt_proj_b': (-4.600166320800781, 0.55),
     'L1_conv_D': (1.0, 0.2),
     'L1_conv_ln_gamma': (1.0, 0.2),
     'L1_conv_ln_beta': (0.0, 0.1),
     'L1_ffn_gate_b': (0.0, 0.1),
     'L1_ffn_b1': (0.0, 0.296),
     'L1_ffn_b2': (0.0, 0.1)}
    factors = {'L0_ffn_c_fc_1': 8.0,
     'L0_ffn_c_fc_2': 8.0,
     'L0_ffn_c_proj_1': 8.0,
     'L0_ffn_c_proj_2': 8.0,
     'L1_conv_A_log': 2.765}
    for name, (base, spread) in spreads.items():
        noise = np.random.default_rng([zlib.crc32(name.encode()), seed]).standard_normal(out[name].shape)
        drawn = base * np.exp(spread * noise) if base else spread * noise
        out[name] = jnp.asarray(drawn.astype(out[name].dtype))
    for name, factor in factors.items():
        out[name] = (out[name] * factor).astype(out[name].dtype)
    return out
```

```python
from contextlib import ExitStack

import numpy as np

import concourse.bass as bass
import concourse.mybir as mybir

ALU = mybir.AluOpType
ACT = mybir.ActivationFunctionType
AX = mybir.AxisListType
F32 = mybir.dt.float32
F32R = mybir.dt.float32r
BF16 = mybir.dt.bfloat16

P = 128
B, C, HH, WW = 4, 384, 32, 32
L = HH * WW
CT = C // P
HALF = 512
NH = L // HALF
N = 16
K0, R0 = 4, 12
DI, R1 = 768, 24
DT1 = DI // P
GROUPS1 = DT1 // CT
BC = 2 * N
TAPS = 4
FF, RANK = 1536, 32
FT = FF // P
KR = C // RANK
E, HID = 4, 1536
HT = HID // P
SLICE = 3
SLICES = HT // SLICE
TT = L // P

VEC = {}
_at = 0
for _name, _n in [("dtb0", K0 * CT), ("D0", K0 * CT), ("dtb1", DT1), ("D1", DT1), ("conv_w", DT1 * TAPS),
                  ("conv_b", DT1), ("ln_w", CT), ("ln_b", CT), ("gamma", CT), ("beta", CT), ("c2", CT),
                  ("gate_b", E), ("b1", E * HT), ("b2", E * CT), ("gate_w", CT * E)]:
    VEC[_name] = (_at, _at + _n)
    _at += _n
VEC_N = _at


def cols(c):
    return slice(c * HALF, (c + 1) * HALF)


def over_tiles(ap, n=CT):
    return ap.unsqueeze(1).to_broadcast([ap.shape[0], n, ap.shape[1]])


class Named(dict):

    __getattr__ = dict.__getitem__


def tensors(nc, stack, table):
    return {name: stack.enter_context(nc.sbuf_tensor(name, shape, dt)) for name, shape, dt in table}


def semaphores(nc, stack, stage, *signals):
    named = {s: stack.enter_context(nc.semaphore(f"{stage}_{s}")) for s in signals}
    return Named(all=list(named.values()), **named)


class Program:
    def __init__(self, nc, io):
        self.nc, self.io = nc, io
        self.last = None

    def clear_last(self, eng, stage):
        if self.last is not None:
            for s in self.last.all:
                eng.sem_clear(s)
        self.last = stage


def load_weights(p, m, st):
    nc, io = p.nc, p.io
    with nc.Block() as block:
        @block.sync
        def _(eng):
            eng.dma_start(m.ident[:, :], io["ident"]).then_inc(st.small, 16)
            eng.dma_start(m.mean_mat[:, :], io["mean_mat"]).then_inc(st.small, 16)
            eng.dma_start(m.pick[:, :], io["pick"]).then_inc(st.small, 16)
            eng.dma_start(m.vec[:, :], io["vec"]).then_inc(st.small, 16)
            eng.dma_start(m.kmask[:, :, :], io["kmask"]).then_inc(st.small, 16)
            eng.dma_start(m.emask[0:RANK, :], io["emask"]).then_inc(st.small, 16)
            eng.dma_start(m.c2p[0:RANK, :], io["c2p"]).then_inc(st.small, 16)
            eng.dma_start(m.A0[:, :], io["A0"]).then_inc(st.alog, 16)
            eng.dma_start(m.A1[:, :], io["A1"]).then_inc(st.alog, 16)
            eng.dma_start(m.w0x[:, :, :, :], io["w0x"]).then_inc(st.big, 16)
            eng.dma_start(m.lowk[96:96 + R0, 0:K0 * C], io["dtw0"]).then_inc(st.big, 16)
            eng.dma_start(m.lowk[96:96 + R1, K0 * C:K0 * C + DI], io["dtw1"]).then_inc(st.big, 16)
            eng.dma_start(m.lowk[0:RANK, 0:FF], io["fc1"]).then_inc(st.big, 16)
            eng.dma_start(m.proj1[:, :, :], io["proj1"]).then_inc(st.big, 16)
            eng.dma_start(m.w_in[:, :, :], io["w_in"]).then_inc(st.big, 16)
            eng.dma_start(m.w1x[:, :, :], io["w1x"]).then_inc(st.big, 16)
            eng.dma_start(m.w_out[:, :, :], io["w_out"]).then_inc(st.big, 16)
            eng.wait_ge(st.big, 16 * 8)
            p.clear_last(eng, st)

        @block.vector
        def _(eng):
            eng.memset(m.zeros[:, :], 0.0).then_inc(st.own, 1)
            eng.memset(m.eps5[:, :], 1e-5).then_inc(st.own, 1)
            eng.memset(m.eps6[:, :], 1e-6).then_inc(st.own, 1)
            eng.wait_ge(st.small, 16 * 7)
            for kt in range(CT):
                a = VEC["c2"][0] + kt
                eng.tensor_scalar(m.kin[:, kt, :], m.kmask[:, kt, :], m.vec[:, a:a + 1], None,
                                  ALU.mult).then_inc(st.own, 1)
            eng.tensor_tensor(m.kout[0:RANK, :], m.emask[0:RANK, :], m.c2p[0:RANK, :],
                              ALU.mult).then_inc(st.own, 1)
            eng.wait_ge(st.exped, 2)
            eng.tensor_scalar(m.A0[:, :], m.A0[:, :], -1.0, None, ALU.mult).then_inc(st.own, 1)
            eng.tensor_scalar(m.A1[:, :], m.A1[:, :], -1.0, None, ALU.mult).then_inc(st.own, 1)

        @block.scalar
        def _(eng):
            eng.wait_ge(st.alog, 32)
            eng.activation(m.A0[:, :], m.A0[:, :], ACT.Exp).then_inc(st.exped, 1)
            eng.activation(m.A1[:, :], m.A1[:, :], ACT.Exp).then_inc(st.exped, 1)


def layer_norm(p, m, st, src, dst, sq, rstd, eps, load=None):
    nc, ps = p.nc, m.ps
    with nc.Block() as block:
        @block.sync
        def _(eng):
            p.clear_last(eng, st)
            if load is not None:
                for c in range(NH):
                    eng.dma_start(src[:, :, cols(c)], load[:, :, cols(c)]).then_inc((st.loaded0, st.loaded1)[c], 16)

        @block.tensor
        def _(eng):
            for c in range(NH):
                if load is not None:
                    eng.wait_ge((st.loaded0, st.loaded1)[c], 16)
                for k in range(CT):
                    mm = eng.matmul(ps[:, c, :], m.mean_mat[:, :], src[:, k, cols(c)], start=k == 0, stop=k == CT - 1)
                mm.then_inc(st.mean, 1)
            for c in range(NH):
                eng.wait_ge(st.squared, c + 1)
                for k in range(CT):
                    mm = eng.matmul(ps[:, 2 + c, :], m.mean_mat[:, :], sq[:, k, cols(c)], start=k == 0, stop=k == CT - 1)
                mm.then_inc(st.variance, 1)

        @block.vector
        def _(eng):
            for c in range(NH):
                eng.wait_ge(st.mean, c + 1)
                eng.tensor_tensor(dst[:, :, cols(c)], src[:, :, cols(c)], over_tiles(ps[:, c, :]),
                                  ALU.subtract).then_inc(st.centred, 1)
            for c in range(NH):
                eng.wait_ge(st.rstd, c + 1)
                eng.wait_ge(st.centred, c + 1)
                eng.tensor_tensor(dst[:, :, cols(c)], dst[:, :, cols(c)], over_tiles(rstd[:, cols(c)]),
                                  ALU.mult).then_inc(st.normed, 1)

        @block.scalar
        def _(eng):
            for c in range(NH):
                eng.wait_ge(st.centred, c + 1)
                eng.activation(sq[:, :, cols(c)], dst[:, :, cols(c)], ACT.Square).then_inc(st.squared, 1)
            for c in range(NH):
                eng.wait_ge(st.variance, c + 1)
                eng.activation(rstd[:, cols(c)], ps[:, 2 + c, :], ACT.Ln, bias=eps[:, :]).then_inc(st.logged, 1)
                eng.wait_ge(st.logged, c + 1)
                eng.activation(rstd[:, cols(c)], rstd[:, cols(c)], ACT.Exp, scale=-0.5).then_inc(st.rstd, 1)


def turn_image(p, m, st, u, ut):
    with p.nc.Block() as block:
        @block.sync
        def _(eng):
            p.clear_last(eng, st)

        @block.gpsimd
        def _(eng):
            eng.tensor_copy(ut[:, 0, :].rearrange("p (w h) -> p w h", w=WW),
                            u[:, 0, :].rearrange("p (h w) -> p w h", w=WW)).then_inc(st.turned, 1)

        @block.vector
        def _(eng):
            for k in range(1, CT):
                eng.tensor_copy(ut[:, k, :].rearrange("p (w h) -> p w h", w=WW),
                                u[:, k, :].rearrange("p (h w) -> p w h", w=WW)).then_inc(st.turned, 1)


def scan_inputs(p, m, st, u, wx, kts, rank, dt_at, bias, D, project=True):
    nc, ps = p.nc, m.ps
    low = m.low
    with nc.Block() as block:
        @block.sync
        def _(eng):
            p.clear_last(eng, st)

        @block.tensor
        def _(eng):
            if project:
                for c in range(NH):
                    for k, src in enumerate(kts):
                        mm = eng.matmul(ps[0:96 + rank, c, :], wx(k), src[:, cols(c)],
                                        start=k == 0, stop=k == len(kts) - 1)
                    mm.then_inc(st.projected, 1)
                eng.wait_ge(st.low, 1)
            for j in range(CT):
                for c in range(NH):
                    a = dt_at + j * P
                    mm = eng.matmul(ps[:, 2 + 2 * j + c, :], m.lowk[96:96 + rank, a:a + P],
                                    low[96:96 + rank, cols(c)], start=True, stop=True)
                mm.then_inc(st.dt, 1)

        @block.scalar
        def _(eng):
            if project:
                eng.wait_ge(st.projected, NH)
                eng.activation(low[96:96 + rank, :].rearrange("p (c n) -> p c n", c=NH), ps[96:96 + rank, 0:NH, :],
                               ACT.Copy).then_inc(st.low, 1)
            for j in range(CT):
                eng.wait_ge(st.dt, j + 1)
                x = ps[:, 2 + 2 * j:4 + 2 * j, :]
                v = m.dA[:, j, :].rearrange("p (c n) -> p c n", c=NH)
                eng.activation(v, x, ACT.Abs, bias=m.vec[:, bias + j:bias + j + 1]).then_inc(st.absed, 1)
            for j in range(CT):
                eng.wait_ge(st.absed, j + 1)
                eng.activation(m.h[:, j, :], m.dA[:, j, :], ACT.Exp, scale=-1.0).then_inc(st.exped, 1)
            for j in range(CT):
                eng.wait_ge(st.exped, j + 1)
                eng.activation(m.dA[:, j, :], m.h[:, j, :], ACT.Ln, bias=1.0).then_inc(st.logged, 1)

        @block.vector
        def _(eng):
            if project:
                eng.wait_ge(st.projected, NH)
                x = ps[0:96, 0:NH, :].rearrange("p c n -> p (c n)")
                eng.tensor_copy(m.parts[0:96, :], x).then_inc(st.split, 1)
                eng.wait_ge(st.split, 1)
                eng.tensor_tensor(low[0:96, :], x, m.parts[0:96, :], ALU.subtract).then_inc(st.split, 1)
                eng.wait_ge(st.split, 2)
                eng.tensor_copy(m.parts[32:64, :], low[32:64, :]).then_inc(st.split, 1)
                eng.tensor_copy(m.parts[64:96, :], low[64:96, :]).then_inc(st.split, 1)
                eng.wait_ge(st.split, 4)
                eng.tensor_tensor(low[64:96, :], low[64:96, :], m.parts[64:96, :], ALU.subtract).then_inc(st.split, 1)
                eng.wait_ge(st.split, 5)
                eng.tensor_copy(m.parts[64:96, :], low[64:96, :]).then_inc(st.split, 1)
            for j in range(CT):
                eng.tensor_scalar(m.diagD[:, j, :], m.ident[:, :], m.vec[:, D + j:D + j + 1], None,
                                  ALU.mult).then_inc(st.diag, 1)
            for j in range(CT):
                eng.wait_ge(st.dt, j + 1)
                eng.wait_ge(st.absed, j + 1)
                eng.tensor_scalar(m.prod[:, j, :].rearrange("p (c n) -> p c n", c=NH), ps[:, 2 + 2 * j:4 + 2 * j, :],
                                  m.vec[:, bias + j:bias + j + 1], 0.0, ALU.add, ALU.max).then_inc(st.relued, 1)
            for j in range(CT):
                eng.wait_ge(st.logged, j + 1)
                eng.wait_ge(st.relued, j + 1)
                eng.tensor_tensor(m.delta[:, j, :], m.dA[:, j, :], m.prod[:, j, :], ALU.add).then_inc(st.delta, 1)

        @block.gpsimd
        def _(eng):
            for j in range(CT):
                eng.wait_ge(st.delta, j + 1)
                eng.tensor_tensor(m.du[:, j, :], m.delta[:, j, :], u(j), ALU.mult).then_inc(st.du, 1)


def selective_scan(p, m, st, u, A, a_at, reverse, take):
    nc, ps = p.nc, m.ps
    PAIRS = N // 2
    SCAN0, EVAC0, PROD0, DBU0, SUM0 = 3, 1, 6, 6, 3
    flip = (lambda ap: ap[:, ::-1]) if reverse else (lambda ap: ap)

    with nc.Block() as block:
        @block.sync
        def _(eng):
            p.clear_last(eng, st)

        @block.scalar
        def _(eng):
            eng.sem_inc(st.evacuated, EVAC0)

            def evacuate(q, i):
                for r, (ring, used, first) in enumerate(((m.Bb, st.dbu, DBU0), (m.Cb, st.prod, PROD0))):
                    eng.wait_ge(st.broadcast, q * 4 + (2 * i + r + 1))
                    eng.wait_ge(used, q * 6 + (3 * i + first - 3))
                    eng.activation(ring[:, i % 2, :].rearrange("p (c n) -> p c n", c=NH), ps[:, 6:8, :],
                                   ACT.Copy).then_inc(st.evacuated, 1)

            def decay(q, i):
                for j in range(CT):
                    eng.wait_ge(st.scanned, q * 6 + (3 * i + j + 1))
                    at = a_at + (q * 2 + i) * CT + j
                    scale = A[:, at:at + 1] if isinstance(at, int) else A[:, bass.ds(at, 1)]
                    eng.activation(m.dA[:, j, :], m.delta[:, j, :], ACT.Exp, scale=scale).then_inc(st.decay, 1)

            evacuate(0, 0)
            with eng.Fori(0, PAIRS - 1) as q:
                decay(q, 0)
                evacuate(q, 1)
                decay(q, 1)
                evacuate(q + 1, 0)
            decay(PAIRS - 1, 0)
            evacuate(PAIRS - 1, 1)
            decay(PAIRS - 1, 1)

        @block.gpsimd
        def _(eng):
            eng.sem_inc(st.dbu, DBU0)

            def drive(q, i):
                eng.wait_ge(st.evacuated, q * 4 + (2 * i + 1 + EVAC0))
                for j in range(CT):
                    eng.wait_ge(st.scanned, q * 6 + (3 * i + j + 1))
                    eng.tensor_tensor(m.dBu[:, j, :], m.du[:, j, :], m.Bb[:, i, :], ALU.mult).then_inc(st.dbu, 1)

            with eng.Fori(0, PAIRS) as q:
                drive(q, 0)
                drive(q, 1)

        @block.vector
        def _(eng):
            eng.sem_inc(st.scanned, SCAN0)
            eng.sem_inc(st.prod, PROD0)

            def scan(q, s):
                j = s % CT
                eng.wait_ge(st.decay, q * 6 + (s + 1))
                eng.wait_ge(st.dbu, q * 6 + (s + 1 + DBU0))
                eng.wait_ge(st.prod, q * 6 + (s - 3 + 1 + PROD0))
                eng.tensor_tensor_scan(flip(m.h[:, j, :]), flip(m.dA[:, j, :]), flip(m.dBu[:, j, :]), 0.0,
                                       ALU.mult, ALU.add).then_inc(st.scanned, 1)

            def weigh(q, s):
                j = s % CT
                if j == 0:
                    eng.wait_ge(st.evacuated, q * 4 + (2 * (s // CT) + 2 + EVAC0))
                eng.wait_ge(st.scanned, q * 6 + (s + 1 + SCAN0))
                eng.wait_ge(st.summed, q * 6 + (s + 1))
                eng.tensor_tensor(m.prod[:, j, :], m.h[:, j, :], m.Cb[:, s // CT, :], ALU.mult).then_inc(st.prod, 1)

            with eng.Fori(0, PAIRS) as q:
                scan(q, 0)
                for s in range(1, 2 * CT):
                    scan(q, s)
                    weigh(q, s - 1)
                weigh(q, 2 * CT - 1)
            take(eng)

        @block.tensor
        def _(eng):
            eng.sem_inc(st.summed, SUM0)

            def broadcast(q, i):
                for r in range(2):
                    eng.wait_ge(st.evacuated, q * 4 + (2 * i + r + EVAC0))
                    at = r * N + q * 2 + i
                    lhs = m.pick[0:96, at:at + 1] if isinstance(at, int) else m.pick[0:96, bass.ds(at, 1)]
                    for c in range(NH):
                        mm = eng.matmul(ps[:, 6 + c, :], lhs.to_broadcast([96, P]), m.parts[0:96, cols(c)],
                                        start=True, stop=True)
                    mm.then_inc(st.broadcast, 1)

            def add(q, i):
                for j in range(CT):
                    eng.wait_ge(st.prod, q * 6 + (3 * i + j + 1 + PROD0))
                    for c in range(NH):
                        mm = eng.matmul(ps[:, 2 * j + c, :], m.ident[:, :], m.prod[:, j, cols(c)],
                                        start=False, stop=False, skip_group_check=True)
                    mm.then_inc(st.summed, 1)

            for b in range(2 * CT):
                eng.matmul(ps[:, b, :], m.zeros[:, 0:P], m.zeros[:, :], start=True, stop=False, skip_group_check=True)
            broadcast(0, 0)
            with eng.Fori(0, PAIRS - 1) as q:
                broadcast(q, 1)
                add(q, 0)
                broadcast(q + 1, 0)
                add(q, 1)
            broadcast(PAIRS - 1, 1)
            add(PAIRS - 1, 0)
            add(PAIRS - 1, 1)
            for j in range(CT):
                for c in range(NH):
                    mm = eng.matmul(ps[:, 2 * j + c, :], m.diagD[:, j, :], u(j)[:, cols(c)],
                                    start=False, stop=True, skip_group_check=True)
                mm.then_inc(st.y, 1)


def gated_residual(p, m, st, y):
    with p.nc.Block() as block:
        @block.sync
        def _(eng):
            p.clear_last(eng, st)

        @block.scalar
        def _(eng):
            for k in range(CT):
                w, b = VEC["ln_w"][0] + k, VEC["ln_b"][0] + k
                eng.activation(y[:, k, :], y[:, k, :], ACT.Gelu, bias=m.vec[:, b:b + 1],
                               scale=m.vec[:, w:w + 1]).then_inc(st.gelu, 1)

        @block.vector
        def _(eng):
            for k in range(CT):
                eng.wait_ge(st.gelu, k + 1)
                eng.tensor_tensor(m.x[:, k, :], m.x[:, k, :], y[:, k, :], ALU.add).then_inc(st.added, 1)


def kron_ffn(p, m, st, u):
    nc, ps = p.nc, m.ps
    z, g, hbuf = m.Bb[:, 0, :], m.Bb[:, 1, :], m.prod[:, :, :].rearrange("p a (b n) -> p (a b) n", n=HALF)
    SLOTS = 4
    with nc.Block() as block:
        @block.sync
        def _(eng):
            p.clear_last(eng, st)

        @block.tensor
        def _(eng):
            for c in range(NH):
                for k in range(CT):
                    mm = eng.matmul(ps[0:RANK, c, :], m.kin[:, k, :], u[:, k, cols(c)], start=k == 0, stop=k == CT - 1)
                mm.then_inc(st.narrow, 1)
            for c in range(NH):
                eng.wait_ge(st.z, c + 1)

                def up(f):
                    s = c * FT + f
                    if s >= SLOTS:
                        eng.wait_ge(st.gelu, s - SLOTS + 1)
                    eng.matmul(ps[:, 2 + s % SLOTS, :], m.lowk[0:RANK, f * P:(f + 1) * P], z[0:RANK, cols(c)],
                               start=True, stop=True).then_inc(st.up, 1)

                def down(f):
                    eng.wait_ge(st.gelu, c * FT + f + 1)
                    eng.matmul(ps[0:RANK, 6 + c, :], m.proj1[:, f, :], hbuf[:, (c * FT + f) % SLOTS, :],
                               start=f == 0, stop=f == FT - 1).then_inc(st.down, 1)

                up(0)
                up(1)
                for f in range(FT):
                    if f + 2 < FT:
                        up(f + 2)
                    down(f)
            for c in range(NH):
                eng.wait_ge(st.g, c + 1)
                for k in range(CT):
                    s = c * CT + k
                    if s >= 2:
                        eng.wait_ge(st.added, s - 1)
                    eng.matmul(ps[:, s % 2, :], m.kout[0:RANK, k * P:(k + 1) * P], g[0:RANK, cols(c)],
                               start=True, stop=True).then_inc(st.wide, 1)

        @block.scalar
        def _(eng):
            for s in range(NH * FT):
                eng.wait_ge(st.up, s + 1)
                if s >= SLOTS:
                    eng.wait_ge(st.down, s - SLOTS + 1)
                eng.activation(hbuf[:, s % SLOTS, :], ps[:, 2 + s % SLOTS, :], ACT.Gelu).then_inc(st.gelu, 1)

        @block.vector
        def _(eng):
            for c in range(NH):
                eng.wait_ge(st.narrow, c + 1)
                eng.tensor_copy(z[0:RANK, cols(c)], ps[0:RANK, c, :]).then_inc(st.z, 1)
            for c in range(NH):
                eng.wait_ge(st.down, (c + 1) * FT)
                eng.tensor_copy(g[0:RANK, cols(c)], ps[0:RANK, 6 + c, :]).then_inc(st.g, 1)
            for c in range(NH):
                for k in range(CT):
                    s = c * CT + k
                    eng.wait_ge(st.wide, s + 1)
                    eng.tensor_tensor(m.x[:, k, cols(c)], m.x[:, k, cols(c)], ps[:, s % 2, :], ALU.add).then_inc(st.added, 1)


def in_projection(p, m, st, u, xin, z):
    nc, ps = p.nc, m.ps
    SETS = 4
    acc = m.dBu
    with nc.Block() as block:
        @block.sync
        def _(eng):
            p.clear_last(eng, st)

        @block.tensor
        def _(eng):
            for f in range(2 * DT1):
                if f >= SETS:
                    t = (f - SETS) // 2
                    eng.wait_ge(st.silu_z if f % 2 else st.tap, t + 1 if f % 2 else TAPS * (t + 1))
                w = (f // 2) * P + (DI if f % 2 else 0)
                for c in range(NH):
                    for k in range(CT):
                        mm = eng.matmul(ps[:, 2 * (f % SETS) + c, :], m.w_in[:, k, w:w + P], u[:, k, cols(c)],
                                        start=k == 0, stop=k == CT - 1)
                mm.then_inc(st.product, 1)

        @block.vector
        def _(eng):
            for t in range(DT1):
                f = 2 * t
                x = ps[:, 2 * (f % SETS):2 * (f % SETS) + 2, :].rearrange("p c n -> p (c n)")
                a = acc[:, t % 3, :]
                w, b = VEC["conv_w"][0] + t * TAPS, VEC["conv_b"][0] + t
                eng.wait_ge(st.product, f + 1)
                if t >= 3:
                    eng.wait_ge(st.silu_x, t - 2)
                eng.tensor_scalar(a, x, m.vec[:, w + TAPS - 1:w + TAPS], m.vec[:, b:b + 1], ALU.mult,
                                  ALU.add).then_inc(st.tap, 1)
                for s in range(1, TAPS):
                    eng.wait_ge(st.tap, TAPS * t + s)
                    i = eng.scalar_tensor_tensor(out=a[:, s:L], in0=x[:, 0:L - s], scalar=m.vec[:, w + TAPS - 1 - s:w + TAPS - s],
                                                 in1=a[:, s:L], op0=ALU.mult, op1=ALU.add)
                    i.then_inc(st.tap, 1)

        @block.scalar
        def _(eng):
            for t in range(DT1):
                f = 2 * t + 1
                eng.wait_ge(st.product, f + 1)
                eng.activation(z[:, t, :].rearrange("p (c n) -> p c n", c=NH), ps[:, 2 * (f % SETS):2 * (f % SETS) + 2, :],
                               ACT.Silu).then_inc(st.silu_z, 1)
                eng.wait_ge(st.tap, TAPS * (t + 1))
                eng.activation(xin[:, t, :], acc[:, t % 3, :], ACT.Silu).then_inc(st.silu_x, 1)


def out_projection(p, m, st, yz, out):
    nc, ps = p.nc, m.ps
    with nc.Block() as block:
        @block.sync
        def _(eng):
            p.clear_last(eng, st)

        @block.tensor
        def _(eng):
            for f in range(CT):
                for c in range(NH):
                    for k in range(DT1):
                        mm = eng.matmul(ps[:, 2 * f + c, :], m.w_out[:, k, f * P:(f + 1) * P], yz[:, k, cols(c)],
                                        start=k == 0, stop=k == DT1 - 1)
                mm.then_inc(st.product, 1)

        @block.scalar
        def _(eng):
            for f in range(CT):
                eng.wait_ge(st.product, f + 1)
                eng.activation(out[:, f, :].rearrange("p (c n) -> p c n", c=NH), ps[:, 2 * f:2 * f + 2, :],
                               ACT.Copy).then_inc(st.copied, 1)


def affine_residual(p, m, st, y):
    with p.nc.Block() as block:
        @block.sync
        def _(eng):
            p.clear_last(eng, st)

        @block.vector
        def _(eng):
            for k in range(CT):
                g, b = VEC["gamma"][0] + k, VEC["beta"][0] + k
                eng.tensor_scalar(y[:, k, :], y[:, k, :], m.vec[:, g:g + 1], m.vec[:, b:b + 1], ALU.mult,
                                  ALU.add).then_inc(st.scaled, 1)
            for k in range(CT):
                eng.wait_ge(st.scaled, k + 1)
                eng.tensor_tensor(m.x[:, k, :], m.x[:, k, :], y[:, k, :], ALU.add).then_inc(st.added, 1)


def gates(p, m, g, st, u):
    nc, ps = p.nc, m.ps
    gw = m.vec[:, VEC["gate_w"][0]:VEC["gate_w"][1]].rearrange("p (k e) -> p k e", e=E)
    gb = m.vec[:, VEC["gate_b"][0]:VEC["gate_b"][1]]
    pr, rank, t1, t2 = g.probs, g.rank, g.t1, g.t2
    with nc.Block() as block:
        @block.sync
        def _(eng):
            p.clear_last(eng, st)

        @block.tensor
        def _(eng):
            for t in range(TT):
                for k in range(CT):
                    mm = eng.matmul(ps[:, 0, t * E:(t + 1) * E], u[:, k, t * P:(t + 1) * P], gw[:, k, :],
                                    start=k == 0, stop=k == CT - 1)
            mm.then_inc(st.scores, 1)

        @block.scalar
        def _(eng):
            for k in range(CT):
                eng.activation(g.u_hi[:, k, :], u[:, k, :], ACT.Copy).then_inc(st.high, 1)
            eng.wait_ge(st.step, 3)
            eng.activation(pr[:, :, :], pr[:, :, :], ACT.Exp).then_inc(st.exped, 1)

        @block.gpsimd
        def _(eng):
            for k in range(CT):
                eng.wait_ge(st.high, k + 1)
                eng.tensor_tensor(g.u_lo[:, k, :], u[:, k, :], g.u_hi[:, k, :].bitcast(F32), ALU.subtract).then_inc(st.low, 1)

        @block.vector
        def _(eng):
            n = [0]

            def then(ins):
                n[0] += 1
                ins.then_inc(st.step, 1)
                eng.wait_ge(st.step, n[0])

            def each(ap):
                return ap.unsqueeze(2).to_broadcast([P, TT, E])

            eng.wait_ge(st.scores, 1)
            then(eng.tensor_tensor(pr[:, :, :], ps[:, 0, 0:TT * E].rearrange("p (t e) -> p t e", e=E),
                                   gb.unsqueeze(1).to_broadcast([P, TT, E]), ALU.add))
            then(eng.tensor_reduce(t1[:, :], pr[:, :, :], AX.X, ALU.max))
            then(eng.tensor_tensor(pr[:, :, :], pr[:, :, :], each(t1[:, :]), ALU.subtract))
            eng.wait_ge(st.exped, 1)
            then(eng.tensor_reduce(t1[:, :], pr[:, :, :], AX.X, ALU.add))
            then(eng.reciprocal(t2[:, :], t1[:, :]))
            then(eng.tensor_tensor(pr[:, :, :], pr[:, :, :], each(t2[:, :]), ALU.mult))
            for e in range(E):
                first = True
                for o in range(E):
                    if o == e:
                        continue
                    dst = rank[:, :, e] if first else t1[:, :]
                    then(eng.tensor_tensor(dst, pr[:, :, o], pr[:, :, e], ALU.is_ge if o < e else ALU.is_gt))
                    if not first:
                        then(eng.tensor_tensor(rank[:, :, e], rank[:, :, e], t1[:, :], ALU.add))
                    first = False
            then(eng.tensor_scalar(rank[:, :, :], rank[:, :, :], 2.0, None, ALU.is_lt))
            then(eng.tensor_tensor(pr[:, :, :], pr[:, :, :], rank[:, :, :], ALU.mult))
            then(eng.tensor_reduce(t1[:, :], pr[:, :, :], AX.X, ALU.add))
            then(eng.tensor_scalar(t1[:, :], t1[:, :], 1e-9, None, ALU.add))
            then(eng.reciprocal(t2[:, :], t1[:, :]))
            then(eng.tensor_tensor(g.comb[:, :, :], pr[:, :, :], each(t2[:, :]), ALU.mult))


def experts(p, m, g, st, out):
    nc, ps, io = p.nc, m.ps, p.io
    SL = SLICE * P
    UNITS = SLICE * NH
    RING = 2

    def passes(eng, out_ap, w_hi, w_lo, x_hi, x_lo, start, stop):
        eng.matmul(out_ap, w_hi, x_hi, start=start, stop=False, skip_group_check=True)
        eng.matmul(out_ap, w_hi, x_lo, start=False, stop=False, skip_group_check=True)
        return eng.matmul(out_ap, w_lo, x_hi, start=False, stop=stop, skip_group_check=True)

    with nc.Block() as block:
        @block.sync
        def _(eng):
            p.clear_last(eng, st)

            def fetch(e, s, slot):
                eng.dma_start(g.raw1[:, slot, :, :], io["w1"][:, e, :, s * SL:(s + 1) * SL]).then_inc(st.got[slot], 16)
                eng.dma_start(g.raw2[:, slot, :, :], io["w2"][:, e, s * SLICE:(s + 1) * SLICE, :]).then_inc(st.got[slot], 16)

            for e in range(E):
                for s in range(SLICES):
                    i = e * SLICES + s
                    if i >= 2:
                        eng.wait_ge(st.split, 2 * (i - 1))
                    fetch(e, s, i % 2)
            eng.wait_ge(st.added, E * CT * NH)
            eng.dma_start(out, m.x[:, :, :]).then_inc(st.stored, 16)
            eng.wait_ge(st.stored, 16)

        @block.gpsimd
        def _(eng):
            for i in range(E * SLICES):
                slot = i % 2
                eng.wait_ge(st.high, 2 * i + 2)
                eng.wait_ge(st.got[slot], 32 * (i // 2 + 1))
                for raw, hi, lo in ((g.raw1, g.w1_hi, g.w1_lo), (g.raw2, g.w2_hi, g.w2_lo)):
                    if i >= 2:
                        eng.wait_ge(st.down, (i - 1) * UNITS)
                    eng.tensor_tensor(lo[:, slot, :, :], raw[:, slot, :, :], hi[:, slot, :, :].bitcast(F32),
                                      ALU.subtract).then_inc(st.split, 1)

        @block.scalar
        def _(eng):
            def gelu(i, v):
                e, s, u = i // SLICES, i % SLICES, i * UNITS + v
                t = s * SLICE + v // NH
                b = VEC["b1"][0] + e * HT + t
                eng.wait_ge(st.hidden, u + 1)
                if u >= RING:
                    eng.wait_ge(st.h_split, u - RING + 1)
                eng.activation(g.hid[:, u % RING, :], ps[:, 6 + u % 2, :], ACT.Gelu,
                               bias=m.vec[:, b:b + 1]).then_inc(st.gelu, 1)

            def high(i):
                slot = i % 2
                eng.wait_ge(st.got[slot], 32 * (i // 2 + 1))
                for raw, hi in ((g.raw1, g.w1_hi), (g.raw2, g.w2_hi)):
                    if i >= 2:
                        eng.wait_ge(st.down, (i - 1) * UNITS)
                        eng.wait_ge(st.split, 2 * (i - 1))
                    eng.activation(hi[:, slot, :, :], raw[:, slot, :, :], ACT.Copy).then_inc(st.high, 1)

            high(0)
            high(1)
            for i in range(E * SLICES):
                for v in range(UNITS):
                    gelu(i, v)
                    if v == 1 and 1 <= i < E * SLICES - 1:
                        high(i + 1)

        @block.vector
        def _(eng):
            def comb_rows(e, c):
                for t in range(HALF // P):
                    tile = c * (HALF // P) + t
                    eng.tensor_scalar(g.diag[:, tile, :], m.ident[:, :], g.comb[:, tile, e:e + 1], None,
                                      ALU.mult).then_inc(st.diag, 1)

            def take_rows(e):
                for c in range(NH):
                    eng.wait_ge(st.rows, e * NH + c + 1)
                    eng.tensor_copy(g.row[:, c, :], ps[:, 6 + c, :]).then_inc(st.row_taken, 1)

            for e in range(E):
                if e:
                    eng.wait_ge(st.rows, e * NH)
                    eng.wait_ge(st.added, e * CT * NH)
                for c in range(NH):
                    comb_rows(e, c)
                take_rows(e)
                for i in range(e * SLICES, (e + 1) * SLICES):
                    for v in range(UNITS):
                        u = i * UNITS + v
                        eng.wait_ge(st.gelu, u + 1)
                        if u >= RING:
                            eng.wait_ge(st.down, u - RING + 1)
                        eng.tensor_copy(g.h_hi[:, u % RING, :], g.hid[:, u % RING, :]).then_inc(st.h_high, 1)
                        eng.wait_ge(st.h_high, u + 1)
                        eng.tensor_tensor(g.h_lo[:, u % RING, :], g.hid[:, u % RING, :],
                                          g.h_hi[:, u % RING, :].bitcast(F32), ALU.subtract).then_inc(st.h_split, 1)
                eng.wait_ge(st.down, (e + 1) * SLICES * UNITS)
                for f in range(CT):
                    b = VEC["b2"][0] + e * CT + f
                    for c in range(NH):
                        s = e * CT * NH + f * NH + c
                        if s >= 2:
                            eng.wait_ge(st.added, s - 1)
                        eng.wait_ge(st.row_taken, (e + 1) * NH)
                        eng.scalar_tensor_tensor(out=g.tmp[:, s % 2, :], in0=ps[:, 2 * f + c, :], scalar=m.vec[:, b:b + 1],
                                                 in1=g.row[:, c, :], op0=ALU.add, op1=ALU.mult).then_inc(st.weighed, 1)
                        eng.wait_ge(st.weighed, s + 1)
                        eng.tensor_tensor(m.x[:, f, cols(c)], m.x[:, f, cols(c)], g.tmp[:, s % 2, :],
                                          ALU.add).then_inc(st.added, 1)

        @block.tensor
        def _(eng):
            def rows(e):
                if e:
                    eng.wait_ge(st.gelu, e * SLICES * UNITS)
                for c in range(NH):
                    eng.wait_ge(st.diag, (e * NH + c + 1) * (HALF // P))
                    for t in range(HALF // P):
                        mm = eng.matmul(ps[:, 6 + c, t * P:(t + 1) * P], g.ones[:, :], g.diag[:, c * (HALF // P) + t, :],
                                        start=True, stop=True)
                    mm.then_inc(st.rows, 1)

            def up(i, v):
                slot, u = i % 2, i * UNITS + v
                t, c = v // NH, v % NH
                if v == 0:
                    eng.wait_ge(st.split, 2 * (i + 1))
                if i % SLICES == 0 and v < 2:
                    eng.wait_ge(st.row_taken, (i // SLICES + 1) * NH)
                if u >= 2:
                    eng.wait_ge(st.gelu, u - 1)
                for k in range(CT):
                    w = slice(t * P, (t + 1) * P)
                    mm = passes(eng, ps[:, 6 + u % 2, :], g.w1_hi[:, slot, k, w], g.w1_lo[:, slot, k, w],
                                g.u_hi[:, k, cols(c)], g.u_lo[:, k, cols(c)], k == 0, k == CT - 1)
                mm.then_inc(st.hidden, 1)

            def down(i, v):
                e, s, slot, u = i // SLICES, i % SLICES, i % 2, i * UNITS + v
                t, c = v // NH, v % NH
                if e and s == 0 and v == 0:
                    eng.wait_ge(st.weighed, e * CT * NH)
                eng.wait_ge(st.h_split, u + 1)
                for f in range(CT):
                    w = slice(f * P, (f + 1) * P)
                    mm = passes(eng, ps[:, 2 * f + c, :], g.w2_hi[:, slot, t, w], g.w2_lo[:, slot, t, w],
                                g.h_hi[:, u % RING, :], g.h_lo[:, u % RING, :], s == 0 and t == 0,
                                s == SLICES - 1 and t == SLICE - 1)
                mm.then_inc(st.down, 1)

            for e in range(E):
                rows(e)
                first, last = e * SLICES, (e + 1) * SLICES
                units = [(i, v) for i in range(first, last) for v in range(UNITS)]
                up(*units[0])
                for n, (i, v) in enumerate(units):
                    if n + 1 < len(units):
                        up(*units[n + 1])
                    down(i, v)


def build(nc, io, out):
    with ExitStack() as ctx:
        p = Program(nc, io)
        banks = ctx.enter_context(nc.psum_tensor("banks", [P, 8, HALF], F32))
        resident = tensors(nc, ctx, [
                ("x", [P, CT, L], F32), ("vec", [P, VEC_N], F32), ("ident", [P, P], F32), ("mean_mat", [P, P], F32),
                ("pick", [P, BC], BF16), ("zeros", [P, HALF], BF16), ("eps5", [P, 1], F32), ("eps6", [P, 1], F32),
                ("kin", [P, CT, RANK], F32), ("kout", [P, C], F32), ("A0", [P, K0 * N * CT], F32),
                ("A1", [P, N * DT1], F32), ("w0x", [P, K0, CT, 96 + R0], F32), ("lowk", [P, K0 * C + DI], F32),
                ("proj1", [P, FT, RANK], F32), ("w_in", [P, CT, 2 * DI], F32), ("w1x", [P, DT1, 96 + R1], F32),
                ("w_out", [P, DT1, C], F32)])

        def stage(name, *signals):
            return semaphores(nc, ctx, name, *signals)

        s_load = stage("load", "small", "alog", "big", "own", "exped")
        ln = ("loaded0", "loaded1", "mean", "centred", "squared", "variance", "logged", "rstd", "normed")
        s_norm = [stage("norm_a", *ln), stage("norm_b", *ln)]
        s_turn = stage("turn", "turned")
        s_in = stage("inputs", "projected", "low", "dt", "absed", "exped", "logged", "split", "diag", "relued", "delta", "du")
        s_scan = stage("scan", "evacuated", "broadcast", "decay", "dbu", "scanned", "prod", "summed", "y", "taken")
        s_gelu = stage("gelu", "gelu", "added")
        s_ffn = stage("ffn", "narrow", "z", "up", "gelu", "down", "g", "wide", "added")
        s_xz = stage("xz", "product", "tap", "silu_z", "silu_x")
        s_out = stage("out", "product", "copied")
        s_aff = stage("affine", "scaled", "added")
        s_gate = stage("gate", "scores", "high", "low", "step", "exped")
        s_moe = stage("moe", "got0", "got1", "high", "split", "hidden", "gelu", "h_high", "h_split", "down",
                      "diag", "rows", "row_taken", "weighed", "added", "stored")
        s_moe.got = [s_moe.got0, s_moe.got1]

        with ExitStack() as once:
            m = Named(ps=banks, **resident, **tensors(nc, once, [
                ("kmask", [P, CT, RANK], F32), ("emask", [P, C], F32), ("c2p", [P, C], F32)]))
            load_weights(p, m, s_load)
        with nc.Block() as block:
            @block.sync
            def _(eng):
                p.clear_last(eng, None)

        with nc.Fori(0, B) as b:
            x_in = io["x"][b]
            with ExitStack() as conv:
                m = Named(ps=banks, **resident, **tensors(nc, conv, [
                        ("dA", [P, CT, L], F32), ("dBu", [P, CT, L], F32), ("h", [P, CT, L], F32),
                        ("prod", [P, CT, L], F32), ("delta", [P, CT, L], F32), ("du", [P, CT, L], F32),
                        ("Bb", [P, 2, L], F32), ("Cb", [P, 2, L], F32), ("parts", [P, L], BF16), ("low", [P, L], F32),
                        ("diagD", [P, CT, P], F32), ("big", [P, 4 * CT, L], F32)]))
                rstd = m.Cb[:, 0, :]
                u, ut, ys = m.big[:, 0:CT, :], m.big[:, CT:2 * CT, :], m.big[:, 2 * CT:3 * CT, :]

                layer_norm(p, m, s_norm[0], m.x, u, m.prod, rstd, m.eps6, load=x_in)
                turn_image(p, m, s_turn, u, ut)
                for n, k in enumerate((0, 2, 1, 3)):
                    src = ut if k % 2 else u
                    scan_inputs(p, m, s_in, lambda j: src[:, j, :], lambda t: m.w0x[:, k, t, :],
                                [src[:, t, :] for t in range(CT)], R0, k * C, VEC["dtb0"][0] + k * CT,
                                VEC["D0"][0] + k * CT)

                    def take(eng):
                        for j in range(CT):
                            eng.wait_ge(s_scan.y, j + 1)
                            y = m.ps[:, 2 * j:2 * j + 2, :].rearrange("p c n -> p (c n)")
                            if n == 0:
                                eng.tensor_copy(ys[:, j, :], y).then_inc(s_scan.taken, 1)
                            elif k % 2 == 0:
                                eng.tensor_tensor(ys[:, j, :], ys[:, j, :], y, ALU.add).then_inc(s_scan.taken, 1)
                            else:
                                v = ys[:, j, :].rearrange("p (h w) -> p h w", w=WW)
                                eng.tensor_tensor(v, v, y.rearrange("p (w h) -> p h w", w=WW), ALU.add).then_inc(s_scan.taken, 1)

                    selective_scan(p, m, s_scan, lambda j: src[:, j, :], m.A0, k * N * CT, k >= 2, take)
                layer_norm(p, m, s_norm[0], ys, ys, m.prod, rstd, m.eps5)
                gated_residual(p, m, s_gelu, ys)
                layer_norm(p, m, s_norm[0], m.x, m.h, m.prod, rstd, m.eps5)
                kron_ffn(p, m, s_ffn, m.h)

                xin, z = m.big[:, 0:DT1, :], m.big[:, DT1:2 * DT1, :]
                layer_norm(p, m, s_norm[0], m.x, m.h, m.prod, rstd, m.eps6)
                in_projection(p, m, s_xz, m.h, xin, z)
                for half in range(GROUPS1):
                    t0 = half * CT
                    scan_inputs(p, m, s_in, lambda j: xin[:, t0 + j, :], lambda t: m.w1x[:, t, :],
                                [xin[:, t, :] for t in range(DT1)], R1, K0 * C + t0 * P, VEC["dtb1"][0] + t0,
                                VEC["D1"][0] + t0, project=half == 0)

                    def gate(eng):
                        for j in range(CT):
                            eng.wait_ge(s_scan.y, j + 1)
                            y = m.ps[:, 2 * j:2 * j + 2, :].rearrange("p c n -> p (c n)")
                            eng.tensor_tensor(z[:, t0 + j, :], z[:, t0 + j, :], y, ALU.mult).then_inc(s_scan.taken, 1)

                    selective_scan(p, m, s_scan, lambda j: xin[:, t0 + j, :], m.A1, half * N * CT, False, gate)
                out_projection(p, m, s_out, z, m.h)
                layer_norm(p, m, s_norm[0], m.h, m.h, m.prod, rstd, m.eps5)
                affine_residual(p, m, s_aff, m.h)

            with ExitStack() as moe:
                SL = SLICE * P
                m = Named(ps=banks, **resident)
                g = Named(**tensors(nc, moe, [
                        ("un", [P, CT, L], F32), ("sq", [P, CT, L], F32), ("rstd", [P, L], F32),
                        ("u_hi", [P, CT, L], F32R), ("u_lo", [P, CT, L], F32R),
                        ("raw1", [P, 2, CT, SL], F32), ("raw2", [P, 2, SLICE, C], F32),
                        ("w1_hi", [P, 2, CT, SL], F32R), ("w1_lo", [P, 2, CT, SL], F32R),
                        ("w2_hi", [P, 2, SLICE, C], F32R), ("w2_lo", [P, 2, SLICE, C], F32R),
                        ("hid", [P, 2, HALF], F32), ("h_hi", [P, 2, HALF], F32R), ("h_lo", [P, 2, HALF], F32R),
                        ("row", [P, NH, HALF], F32), ("tmp", [P, 2, HALF], F32), ("diag", [P, TT, P], F32),
                        ("ones", [P, P], F32), ("probs", [P, TT, E], F32), ("rank", [P, TT, E], F32),
                        ("comb", [P, TT, E], F32), ("t1", [P, TT], F32), ("t2", [P, TT], F32)]))
                layer_norm(p, m, s_norm[1], m.x, g.un, g.sq, g.rstd, m.eps5)
                with nc.Block() as block:
                    @block.sync
                    def _(eng):
                        p.clear_last(eng, None)

                    @block.vector
                    def _(eng):
                        eng.memset(g.ones[:, :], 1.0)
                gates(p, m, g, s_gate, g.un)
                experts(p, m, g, s_moe, out[b])
            with nc.Block() as block:
                @block.sync
                def _(eng):
                    p.clear_last(eng, None)


def kernel(**inputs):
    import concourse.bacc as bacc
    import ml_dtypes
    from concourse.bass_utils import run_bass_kernel_spmd

    a = {k: np.asarray(v) for k, v in inputs.items()}

    def rows(v, t):
        return v.reshape(t, P, *v.shape[1:]).swapaxes(0, 1)

    wx0 = a["L0_conv_x_proj_weight"]
    bc = wx0[:, R0:]
    wx0 = np.concatenate([bc, bc, bc, wx0[:, :R0]], axis=1).transpose(2, 0, 1)
    wx1 = a["L1_conv_x_proj_w"]
    bc = wx1[R1:]
    wx1 = np.concatenate([bc, bc, bc, wx1[:R1]], axis=0).T
    vec = {
        "dtb0": a["L0_conv_dt_projs_bias"].reshape(K0 * CT, P).T, "D0": a["L0_conv_Ds"].reshape(K0 * CT, P).T,
        "dtb1": a["L1_conv_dt_proj_b"].reshape(DT1, P).T, "D1": a["L1_conv_D"].reshape(DT1, P).T,
        "conv_w": rows(a["L1_conv_conv_w"], DT1).reshape(P, -1), "conv_b": a["L1_conv_conv_b"].reshape(DT1, P).T,
        "ln_w": a["L0_conv_ln_weight"].reshape(CT, P).T, "ln_b": a["L0_conv_ln_bias"].reshape(CT, P).T,
        "gamma": a["L1_conv_ln_gamma"].reshape(CT, P).T, "beta": a["L1_conv_ln_beta"].reshape(CT, P).T,
        "c2": np.tile(a["L0_ffn_c_fc_2"][0], RANK).reshape(CT, P).T,
        "gate_b": np.tile(a["L1_ffn_gate_b"][None], (P, 1)),
        "b1": a["L1_ffn_b1"].reshape(E * HT, P).T, "b2": a["L1_ffn_b2"].reshape(E * CT, P).T,
        "gate_w": rows(a["L1_ffn_gate_w"], CT).reshape(P, -1),
    }
    block = np.arange(C)[:, None] // KR == np.arange(RANK)[None]
    arrays = {
        "x": a["x"].reshape(B, CT, P, L).transpose(0, 2, 1, 3),
        "ident": np.eye(P, dtype=np.float32),
        "mean_mat": np.full((P, P), 1.0 / C, np.float32),
        "pick": (np.arange(P)[:, None] % BC == np.arange(BC)[None]).astype(ml_dtypes.bfloat16),
        "vec": np.concatenate([vec[n] for n in VEC], axis=1),
        "kmask": rows(block.astype(np.float32), CT), "emask": block.T.astype(np.float32),
        "c2p": np.tile(a["L0_ffn_c_proj_2"][:, 0], (RANK, RANK)),
        "A0": a["L0_conv_A_logs"].reshape(K0, CT, P, N).transpose(2, 0, 3, 1).reshape(P, -1),
        "A1": a["L1_conv_A_log"].reshape(GROUPS1, CT, P, N).transpose(2, 0, 3, 1).reshape(P, -1),
        "w0x": wx0.reshape(CT, P, K0, 96 + R0).transpose(1, 2, 0, 3),
        "dtw0": a["L0_conv_dt_projs_weight"].transpose(2, 0, 1).reshape(R0, K0 * C),
        "dtw1": a["L1_conv_dt_proj_w"].T, "fc1": a["L0_ffn_c_fc_1"].T,
        "proj1": rows(a["L0_ffn_c_proj_1"].T, FT),
        "w_in": rows(a["L1_conv_in_proj_w"].T, CT), "w1x": rows(wx1, DT1),
        "w_out": rows(a["L1_conv_out_proj_w"].T, DT1),
        "w1": a["L1_ffn_w1"].reshape(E, CT, P, HID).transpose(2, 0, 1, 3),
        "w2": a["L1_ffn_w2"].reshape(E, HT, P, C).transpose(2, 0, 1, 3),
    }
    arrays = {f"{n}_in": np.ascontiguousarray(v) for n, v in arrays.items()}
    nc = bacc.Bacc("TRN2", target_bir_lowering=False, num_devices=1)
    io = {n[:-3]: nc.dram_tensor(n, v.shape, mybir.dt.from_np(v.dtype), kind="ExternalInput").ap()
          for n, v in arrays.items()}
    out = nc.dram_tensor("out", (B, P, CT, L), F32, kind="ExternalOutput").ap()
    build(nc, io, out)
    r = run_bass_kernel_spmd(nc, [arrays], core_ids=[0])
    y = r.results[0]["out"]
    return y.transpose(0, 2, 1, 3).reshape(B, C, HH, WW)
```

```python
from contextlib import ExitStack

import numpy as np

import concourse.bass as bass
import concourse.mybir as mybir

ALU = mybir.AluOpType
ACT = mybir.ActivationFunctionType
AX = mybir.AxisListType
F32 = mybir.dt.float32
F32R = mybir.dt.float32r
BF16 = mybir.dt.bfloat16

P = 128
B, C, HH, WW = 4, 384, 32, 32
L = HH * WW
CT = C // P
HALF = 512
NH = L // HALF
N = 16
K0, R0 = 4, 12
DI, R1 = 768, 24
DT1 = DI // P
GROUPS1 = DT1 // CT
BC = 2 * N
TAPS = 4
FF, RANK = 1536, 32
FT = FF // P
KR = C // RANK
E, HID = 4, 1536
HT = HID // P
SLICE = 3
SLICES = HT // SLICE
TT = L // P

VEC = {}
_at = 0
for _name, _n in [("dtb0", K0 * CT), ("D0", K0 * CT), ("dtb1", DT1), ("D1", DT1), ("conv_w", DT1 * TAPS),
                  ("conv_b", DT1), ("ln_w", CT), ("ln_b", CT), ("gamma", CT), ("beta", CT), ("c2", CT),
                  ("gate_b", E), ("b1", E * HT), ("b2", E * CT), ("gate_w", CT * E)]:
    VEC[_name] = (_at, _at + _n)
    _at += _n
VEC_N = _at


def cols(c):
    return slice(c * HALF, (c + 1) * HALF)


def over_tiles(ap, n=CT):
    return ap.unsqueeze(1).to_broadcast([ap.shape[0], n, ap.shape[1]])


class Named(dict):

    __getattr__ = dict.__getitem__


def tensors(nc, stack, table):
    return {name: stack.enter_context(nc.sbuf_tensor(name, shape, dt)) for name, shape, dt in table}


def semaphores(nc, stack, stage, *signals):
    named = {s: stack.enter_context(nc.semaphore(f"{stage}_{s}")) for s in signals}
    return Named(all=list(named.values()), **named)


class Program:
    def __init__(self, nc, io):
        self.nc, self.io = nc, io
        self.last = None

    def clear_last(self, eng, stage):
        if self.last is not None:
            for s in self.last.all:
                eng.sem_clear(s)
        self.last = stage


def load_weights(p, m, st):
    nc, io = p.nc, p.io
    with nc.Block() as block:
        @block.sync
        def _(eng):
            eng.dma_start(m.ident[:, :], io["ident"]).then_inc(st.small, 16)
            eng.dma_start(m.mean_mat[:, :], io["mean_mat"]).then_inc(st.small, 16)
            eng.dma_start(m.pick[:, :], io["pick"]).then_inc(st.small, 16)
            eng.dma_start(m.vec[:, :], io["vec"]).then_inc(st.small, 16)
            eng.dma_start(m.kmask[:, :, :], io["kmask"]).then_inc(st.small, 16)
            eng.dma_start(m.emask[0:RANK, :], io["emask"]).then_inc(st.small, 16)
            eng.dma_start(m.c2p[0:RANK, :], io["c2p"]).then_inc(st.small, 16)
            eng.dma_start(m.A0[:, :], io["A0"]).then_inc(st.alog, 16)
            eng.dma_start(m.A1[:, :], io["A1"]).then_inc(st.alog, 16)
            eng.dma_start(m.w0x[:, :, :, :], io["w0x"]).then_inc(st.big, 16)
            eng.dma_start(m.lowk[96:96 + R0, 0:K0 * C], io["dtw0"]).then_inc(st.big, 16)
            eng.dma_start(m.lowk[96:96 + R1, K0 * C:K0 * C + DI], io["dtw1"]).then_inc(st.big, 16)
            eng.dma_start(m.lowk[0:RANK, 0:FF], io["fc1"]).then_inc(st.big, 16)
            eng.dma_start(m.proj1[:, :, :], io["proj1"]).then_inc(st.big, 16)
            eng.dma_start(m.w_in[:, :, :], io["w_in"]).then_inc(st.big, 16)
            eng.dma_start(m.w1x[:, :, :], io["w1x"]).then_inc(st.big, 16)
            eng.dma_start(m.w_out[:, :, :], io["w_out"]).then_inc(st.big, 16)
            eng.wait_ge(st.big, 16 * 8)
            p.clear_last(eng, st)

        @block.vector
        def _(eng):
            eng.memset(m.zeros[:, :], 0.0).then_inc(st.own, 1)
            eng.memset(m.eps5[:, :], 1e-5).then_inc(st.own, 1)
            eng.memset(m.eps6[:, :], 1e-6).then_inc(st.own, 1)
            eng.wait_ge(st.small, 16 * 7)
            for kt in range(CT):
                a = VEC["c2"][0] + kt
                eng.tensor_scalar(m.kin[:, kt, :], m.kmask[:, kt, :], m.vec[:, a:a + 1], None,
                                  ALU.mult).then_inc(st.own, 1)
            eng.tensor_tensor(m.kout[0:RANK, :], m.emask[0:RANK, :], m.c2p[0:RANK, :],
                              ALU.mult).then_inc(st.own, 1)
            eng.wait_ge(st.exped, 2)
            eng.tensor_scalar(m.A0[:, :], m.A0[:, :], -1.0, None, ALU.mult).then_inc(st.own, 1)
            eng.tensor_scalar(m.A1[:, :], m.A1[:, :], -1.0, None, ALU.mult).then_inc(st.own, 1)
            d = m.vec[:, VEC["D0"][0]:VEC["D0"][1]].rearrange("p (k t) -> p t k", t=CT)
            eng.tensor_reduce(m.Dsum[:, :], d, AX.X, ALU.add).then_inc(st.own, 1)

        @block.scalar
        def _(eng):
            eng.wait_ge(st.alog, 32)
            eng.activation(m.A0[:, :], m.A0[:, :], ACT.Exp).then_inc(st.exped, 1)
            eng.activation(m.A1[:, :], m.A1[:, :], ACT.Exp).then_inc(st.exped, 1)


def layer_norm(p, m, st, src, dst, sq, rstd, eps, load=None):
    nc, ps = p.nc, m.ps
    with nc.Block() as block:
        @block.sync
        def _(eng):
            p.clear_last(eng, st)
            if load is not None:
                for c in range(NH):
                    eng.dma_start(src[:, :, cols(c)], load[:, :, cols(c)]).then_inc((st.loaded0, st.loaded1)[c], 16)

        @block.tensor
        def _(eng):
            for c in range(NH):
                if load is not None:
                    eng.wait_ge((st.loaded0, st.loaded1)[c], 16)
                for k in range(CT):
                    mm = eng.matmul(ps[:, c, :], m.mean_mat[:, :], src[:, k, cols(c)], start=k == 0, stop=k == CT - 1)
                mm.then_inc(st.mean, 1)
            for c in range(NH):
                eng.wait_ge(st.squared, c + 1)
                for k in range(CT):
                    mm = eng.matmul(ps[:, 2 + c, :], m.mean_mat[:, :], sq[:, k, cols(c)], start=k == 0, stop=k == CT - 1)
                mm.then_inc(st.variance, 1)

        @block.vector
        def _(eng):
            for c in range(NH):
                eng.wait_ge(st.mean, c + 1)
                eng.tensor_tensor(dst[:, :, cols(c)], src[:, :, cols(c)], over_tiles(ps[:, c, :]),
                                  ALU.subtract).then_inc(st.centred, 1)
            for c in range(NH):
                eng.wait_ge(st.rstd, c + 1)
                eng.wait_ge(st.centred, c + 1)
                eng.tensor_tensor(dst[:, :, cols(c)], dst[:, :, cols(c)], over_tiles(rstd[:, cols(c)]),
                                  ALU.mult).then_inc(st.normed, 1)

        @block.scalar
        def _(eng):
            for c in range(NH):
                eng.wait_ge(st.centred, c + 1)
                eng.activation(sq[:, :, cols(c)], dst[:, :, cols(c)], ACT.Square).then_inc(st.squared, 1)
            for c in range(NH):
                eng.wait_ge(st.variance, c + 1)
                eng.activation(rstd[:, cols(c)], ps[:, 2 + c, :], ACT.Ln, bias=eps[:, :]).then_inc(st.logged, 1)
                eng.wait_ge(st.logged, c + 1)
                eng.activation(rstd[:, cols(c)], rstd[:, cols(c)], ACT.Exp, scale=-0.5).then_inc(st.rstd, 1)


def turn_image(p, m, st, u, ut):
    with p.nc.Block() as block:
        @block.sync
        def _(eng):
            p.clear_last(eng, st)

        @block.gpsimd
        def _(eng):
            eng.tensor_copy(ut[:, 0, :].rearrange("p (w h) -> p w h", w=WW),
                            u[:, 0, :].rearrange("p (h w) -> p w h", w=WW)).then_inc(st.turned, 1)

        @block.vector
        def _(eng):
            for k in range(1, CT):
                eng.tensor_copy(ut[:, k, :].rearrange("p (w h) -> p w h", w=WW),
                                u[:, k, :].rearrange("p (h w) -> p w h", w=WW)).then_inc(st.turned, 1)


def scan_inputs(p, m, st, u, wx, kts, rank, dt_at, bias, project=True):
    nc, ps = p.nc, m.ps
    low = m.low
    with nc.Block() as block:
        @block.sync
        def _(eng):
            p.clear_last(eng, st)

        @block.tensor
        def _(eng):
            if project:
                for c in range(NH):
                    for k, src in enumerate(kts):
                        mm = eng.matmul(ps[0:96 + rank, c, :], wx(k), src[:, cols(c)],
                                        start=k == 0, stop=k == len(kts) - 1)
                    mm.then_inc(st.projected, 1)
            for j in range(CT):
                for c in range(NH):
                    if project and j == 0:
                        eng.wait_ge(st.low, c + 1)
                    a = dt_at + j * P
                    mm = eng.matmul(ps[:, 2 + 2 * j + c, :], m.lowk[96:96 + rank, a:a + P],
                                    low[96:96 + rank, cols(c)], start=True, stop=True)
                mm.then_inc(st.dt, 1)

        @block.scalar
        def _(eng):
            if project:
                for c in range(NH):
                    eng.wait_ge(st.projected, c + 1)
                    eng.activation(low[96:96 + rank, cols(c)], ps[96:96 + rank, c, :], ACT.Copy).then_inc(st.low, 1)
            for j in range(CT):
                eng.wait_ge(st.dt, j + 1)
                x = ps[:, 2 + 2 * j:4 + 2 * j, :]
                v = m.dA[:, j, :].rearrange("p (c n) -> p c n", c=NH)
                eng.activation(v, x, ACT.Abs, bias=m.vec[:, bias + j:bias + j + 1]).then_inc(st.absed, 1)
                eng.wait_ge(st.absed, j + 1)
                eng.activation(m.h[:, j, :], m.dA[:, j, :], ACT.Exp, scale=-1.0).then_inc(st.exped, 1)
                eng.wait_ge(st.exped, j + 1)
                eng.activation(m.dA[:, j, :], m.h[:, j, :], ACT.Ln, bias=1.0).then_inc(st.logged, 1)

        @block.vector
        def _(eng):
            if project:
                eng.wait_ge(st.projected, NH)
                x = ps[0:96, 0:NH, :].rearrange("p c n -> p (c n)")
                eng.tensor_copy(m.parts[0:96, :], x).then_inc(st.split, 1)
                eng.wait_ge(st.split, 1)
                eng.tensor_tensor(low[0:96, :], x, m.parts[0:96, :], ALU.subtract).then_inc(st.split, 1)
                eng.wait_ge(st.split, 2)
                eng.tensor_copy(m.parts[32:64, :], low[32:64, :]).then_inc(st.split, 1)
                eng.tensor_copy(m.parts[64:96, :], low[64:96, :]).then_inc(st.split, 1)
                eng.wait_ge(st.split, 4)
                eng.tensor_tensor(low[64:96, :], low[64:96, :], m.parts[64:96, :], ALU.subtract).then_inc(st.split, 1)
                eng.wait_ge(st.split, 5)
                eng.tensor_copy(m.parts[64:96, :], low[64:96, :]).then_inc(st.split, 1)
            for j in range(CT):
                eng.wait_ge(st.dt, j + 1)
                eng.wait_ge(st.absed, j + 1)
                eng.tensor_scalar(m.prod[:, j, :].rearrange("p (c n) -> p c n", c=NH), ps[:, 2 + 2 * j:4 + 2 * j, :],
                                  m.vec[:, bias + j:bias + j + 1], 0.0, ALU.add, ALU.max).then_inc(st.relued, 1)
            for j in range(CT):
                eng.wait_ge(st.logged, j + 1)
                eng.wait_ge(st.relued, j + 1)
                eng.tensor_tensor(m.delta[:, j, :], m.dA[:, j, :], m.prod[:, j, :], ALU.add).then_inc(st.delta, 1)
            eng.wait_ge(st.delta, CT)
            eng.tensor_tensor(m.du[:, CT - 1, :], m.delta[:, CT - 1, :], u(CT - 1), ALU.mult).then_inc(st.du, 1)

        @block.gpsimd
        def _(eng):
            for j in range(CT - 1):
                eng.wait_ge(st.delta, j + 1)
                eng.tensor_tensor(m.du[:, j, :], m.delta[:, j, :], u(j), ALU.mult).then_inc(st.du, 1)


def selective_scan(p, m, st, A, a_at, reverse, take):
    nc, ps = p.nc, m.ps
    PAIRS = N // 2
    SCAN0, EVAC0, PROD0, DBU0, SUM0 = 3, 1, 6, 6, 3
    flip = (lambda ap: ap[:, ::-1]) if reverse else (lambda ap: ap)

    with nc.Block() as block:
        @block.sync
        def _(eng):
            p.clear_last(eng, st)

        @block.scalar
        def _(eng):
            eng.sem_inc(st.evacuated, EVAC0)

            def evacuate(q, i, r):
                ring, used, first = ((m.Bb, st.dbu, DBU0), (m.Cb, st.prod, PROD0))[r]
                eng.wait_ge(st.broadcast, q * 4 + (2 * i + r + 1))
                eng.wait_ge(used, q * 6 + (3 * i + first - 3))
                eng.activation(ring[:, i, :].rearrange("p (c n) -> p c n", c=NH), ps[:, 6:8, :],
                               ACT.Copy).then_inc(st.evacuated, 1)

            def decay(q, i, j):
                eng.wait_ge(st.scanned, q * 6 + (3 * i + j + 1))
                at = a_at + (q * 2 + i) * CT + j
                scale = A[:, at:at + 1] if isinstance(at, int) else A[:, bass.ds(at, 1)]
                eng.activation(m.dA[:, j, :], m.delta[:, j, :], ACT.Exp, scale=scale).then_inc(st.decay, 1)

            def turn(q, i, following):
                decay(q, i, 0)
                if following:
                    evacuate(*following, 0)
                decay(q, i, 1)
                decay(q, i, 2)
                if following:
                    evacuate(*following, 1)

            evacuate(0, 0, 0)
            evacuate(0, 0, 1)
            with eng.Fori(0, PAIRS - 1) as q:
                turn(q, 0, (q, 1))
                turn(q, 1, (q + 1, 0))
            turn(PAIRS - 1, 0, (PAIRS - 1, 1))
            turn(PAIRS - 1, 1, None)

        @block.gpsimd
        def _(eng):
            eng.sem_inc(st.dbu, DBU0)

            def drive(q, i):
                eng.wait_ge(st.evacuated, q * 4 + (2 * i + 1 + EVAC0))
                for j in range(CT):
                    eng.wait_ge(st.scanned, q * 6 + (3 * i + j + 1))
                    eng.tensor_tensor(m.dBu[:, j, :], m.du[:, j, :], m.Bb[:, i, :], ALU.mult).then_inc(st.dbu, 1)

            with eng.Fori(0, PAIRS) as q:
                drive(q, 0)
                drive(q, 1)

        @block.vector
        def _(eng):
            eng.sem_inc(st.scanned, SCAN0)
            eng.sem_inc(st.prod, PROD0)

            def scan(q, s):
                j = s % CT
                eng.wait_ge(st.decay, q * 6 + (s + 1))
                eng.wait_ge(st.dbu, q * 6 + (s + 1 + DBU0))
                eng.wait_ge(st.prod, q * 6 + (s - 3 + 1 + PROD0))
                eng.tensor_tensor_scan(flip(m.h[:, j, :]), flip(m.dA[:, j, :]), flip(m.dBu[:, j, :]), 0.0,
                                       ALU.mult, ALU.add).then_inc(st.scanned, 1)

            def weigh(q, s):
                j = s % CT
                if j == 0:
                    eng.wait_ge(st.evacuated, q * 4 + (2 * (s // CT) + 2 + EVAC0))
                eng.wait_ge(st.scanned, q * 6 + (s + 1 + SCAN0))
                eng.wait_ge(st.summed, q * 6 + (s + 1))
                eng.tensor_tensor(m.prod[:, j, :], m.h[:, j, :], m.Cb[:, s // CT, :], ALU.mult).then_inc(st.prod, 1)

            with eng.Fori(0, PAIRS) as q:
                scan(q, 0)
                for s in range(1, 2 * CT):
                    scan(q, s)
                    weigh(q, s - 1)
                weigh(q, 2 * CT - 1)
            for j in range(CT):
                eng.wait_ge(st.summed, SUM0 + N * CT - CT + j + 1)
                take(eng, j, ps[:, 2 * j:2 * j + 2, :].rearrange("p c n -> p (c n)"))

        @block.tensor
        def _(eng):
            eng.sem_inc(st.summed, SUM0)

            def broadcast(q, i, r):
                eng.wait_ge(st.evacuated, q * 4 + (2 * i + r + EVAC0))
                at = r * N + q * 2 + i
                lhs = m.pick[0:96, at:at + 1] if isinstance(at, int) else m.pick[0:96, bass.ds(at, 1)]
                for c in range(NH):
                    mm = eng.matmul(ps[:, 6 + c, :], lhs.to_broadcast([96, P]), m.parts[0:96, cols(c)],
                                    start=True, stop=True)
                mm.then_inc(st.broadcast, 1)

            def add(q, i, j, last=False):
                eng.wait_ge(st.prod, q * 6 + (3 * i + j + 1 + PROD0))
                for c in range(NH):
                    mm = eng.matmul(ps[:, 2 * j + c, :], m.ident[:, :], m.prod[:, j, cols(c)],
                                    start=False, stop=last, skip_group_check=True)
                mm.then_inc(st.summed, 1)

            def turn(q, i, ahead, last=False):
                if ahead:
                    broadcast(*ahead, 0)
                add(q, i, 0, last)
                add(q, i, 1, last)
                if ahead:
                    broadcast(*ahead, 1)
                add(q, i, 2, last)

            for b in range(2 * CT):
                eng.matmul(ps[:, b, :], m.zeros[:, 0:P], m.zeros[:, :], start=True, stop=False, skip_group_check=True)
            for i in range(2):
                for r in range(2):
                    broadcast(0, i, r)
            with eng.Fori(0, PAIRS - 1) as q:
                turn(q, 0, (q + 1, 0))
                turn(q, 1, (q + 1, 1))
            turn(PAIRS - 1, 0, None)
            turn(PAIRS - 1, 1, None, last=True)


def gated_residual(p, m, st, y):
    with p.nc.Block() as block:
        @block.sync
        def _(eng):
            p.clear_last(eng, st)

        @block.scalar
        def _(eng):
            for k in range(CT):
                w, b = VEC["ln_w"][0] + k, VEC["ln_b"][0] + k
                eng.activation(y[:, k, :], y[:, k, :], ACT.Gelu, bias=m.vec[:, b:b + 1],
                               scale=m.vec[:, w:w + 1]).then_inc(st.gelu, 1)

        @block.vector
        def _(eng):
            for k in range(CT):
                eng.wait_ge(st.gelu, k + 1)
                eng.tensor_tensor(m.x[:, k, :], m.x[:, k, :], y[:, k, :], ALU.add).then_inc(st.added, 1)


def kron_ffn(p, m, st, u):
    nc, ps = p.nc, m.ps
    z, g, hbuf = m.Bb[:, 0, :], m.Bb[:, 1, :], m.prod[:, :, :].rearrange("p a (b n) -> p (a b) n", n=HALF)
    SLOTS = 4
    with nc.Block() as block:
        @block.sync
        def _(eng):
            p.clear_last(eng, st)

        @block.tensor
        def _(eng):
            for c in range(NH):
                for k in range(CT):
                    mm = eng.matmul(ps[0:RANK, c, :], m.kin[:, k, :], u[:, k, cols(c)], start=k == 0, stop=k == CT - 1)
                mm.then_inc(st.narrow, 1)
            for c in range(NH):
                eng.wait_ge(st.z, c + 1)

                def up(f):
                    s = c * FT + f
                    if s >= SLOTS:
                        eng.wait_ge(st.gelu, s - SLOTS + 1)
                    eng.matmul(ps[:, 2 + s % SLOTS, :], m.lowk[0:RANK, f * P:(f + 1) * P], z[0:RANK, cols(c)],
                               start=True, stop=True).then_inc(st.up, 1)

                def down(f):
                    eng.wait_ge(st.gelu, c * FT + f + 1)
                    eng.matmul(ps[0:RANK, 6 + c, :], m.proj1[:, f, :], hbuf[:, (c * FT + f) % SLOTS, :],
                               start=f == 0, stop=f == FT - 1).then_inc(st.down, 1)

                up(0)
                up(1)
                for f in range(FT):
                    if f + 2 < FT:
                        up(f + 2)
                    down(f)
            for c in range(NH):
                eng.wait_ge(st.g, c + 1)
                for k in range(CT):
                    s = c * CT + k
                    if s >= 2:
                        eng.wait_ge(st.added, s - 1)
                    eng.matmul(ps[:, s % 2, :], m.kout[0:RANK, k * P:(k + 1) * P], g[0:RANK, cols(c)],
                               start=True, stop=True).then_inc(st.wide, 1)

        @block.scalar
        def _(eng):
            for s in range(NH * FT):
                eng.wait_ge(st.up, s + 1)
                if s >= SLOTS:
                    eng.wait_ge(st.down, s - SLOTS + 1)
                eng.activation(hbuf[:, s % SLOTS, :], ps[:, 2 + s % SLOTS, :], ACT.Gelu).then_inc(st.gelu, 1)

        @block.vector
        def _(eng):
            for c in range(NH):
                eng.wait_ge(st.narrow, c + 1)
                eng.tensor_copy(z[0:RANK, cols(c)], ps[0:RANK, c, :]).then_inc(st.z, 1)
            for c in range(NH):
                eng.wait_ge(st.down, (c + 1) * FT)
                eng.tensor_copy(g[0:RANK, cols(c)], ps[0:RANK, 6 + c, :]).then_inc(st.g, 1)
            for c in range(NH):
                for k in range(CT):
                    s = c * CT + k
                    eng.wait_ge(st.wide, s + 1)
                    eng.tensor_tensor(m.x[:, k, cols(c)], m.x[:, k, cols(c)], ps[:, s % 2, :], ALU.add).then_inc(st.added, 1)


def in_projection(p, m, st, u, xin, z):
    nc, ps = p.nc, m.ps
    SETS = 4
    acc = m.dBu
    with nc.Block() as block:
        @block.sync
        def _(eng):
            p.clear_last(eng, st)

        @block.tensor
        def _(eng):
            for f in range(2 * DT1):
                if f >= SETS:
                    t = (f - SETS) // 2
                    eng.wait_ge(st.silu_z if f % 2 else st.tap, t + 1 if f % 2 else TAPS * (t + 1))
                w = (f // 2) * P + (DI if f % 2 else 0)
                for c in range(NH):
                    for k in range(CT):
                        mm = eng.matmul(ps[:, 2 * (f % SETS) + c, :], m.w_in[:, k, w:w + P], u[:, k, cols(c)],
                                        start=k == 0, stop=k == CT - 1)
                mm.then_inc(st.product, 1)

        @block.vector
        def _(eng):
            for t in range(DT1):
                f = 2 * t
                x = ps[:, 2 * (f % SETS):2 * (f % SETS) + 2, :].rearrange("p c n -> p (c n)")
                a = acc[:, t % 3, :]
                w, b = VEC["conv_w"][0] + t * TAPS, VEC["conv_b"][0] + t
                eng.wait_ge(st.product, f + 1)
                if t >= 3:
                    eng.wait_ge(st.silu_x, t - 2)
                eng.tensor_scalar(a, x, m.vec[:, w + TAPS - 1:w + TAPS], m.vec[:, b:b + 1], ALU.mult,
                                  ALU.add).then_inc(st.tap, 1)
                for s in range(1, TAPS):
                    eng.wait_ge(st.tap, TAPS * t + s)
                    i = eng.scalar_tensor_tensor(out=a[:, s:L], in0=x[:, 0:L - s], scalar=m.vec[:, w + TAPS - 1 - s:w + TAPS - s],
                                                 in1=a[:, s:L], op0=ALU.mult, op1=ALU.add)
                    i.then_inc(st.tap, 1)

        @block.scalar
        def _(eng):
            for t in range(DT1):
                f = 2 * t + 1
                eng.wait_ge(st.product, f + 1)
                eng.activation(z[:, t, :].rearrange("p (c n) -> p c n", c=NH), ps[:, 2 * (f % SETS):2 * (f % SETS) + 2, :],
                               ACT.Silu).then_inc(st.silu_z, 1)
                eng.wait_ge(st.tap, TAPS * (t + 1))
                eng.activation(xin[:, t, :], acc[:, t % 3, :], ACT.Silu).then_inc(st.silu_x, 1)


def out_projection(p, m, st, yz, out):
    nc, ps = p.nc, m.ps
    with nc.Block() as block:
        @block.sync
        def _(eng):
            p.clear_last(eng, st)

        @block.tensor
        def _(eng):
            for f in range(CT):
                for c in range(NH):
                    for k in range(DT1):
                        mm = eng.matmul(ps[:, 2 * f + c, :], m.w_out[:, k, f * P:(f + 1) * P], yz[:, k, cols(c)],
                                        start=k == 0, stop=k == DT1 - 1)
                mm.then_inc(st.product, 1)

        @block.scalar
        def _(eng):
            for f in range(CT):
                eng.wait_ge(st.product, f + 1)
                eng.activation(out[:, f, :].rearrange("p (c n) -> p c n", c=NH), ps[:, 2 * f:2 * f + 2, :],
                               ACT.Copy).then_inc(st.copied, 1)


def affine_residual(p, m, st, y):
    with p.nc.Block() as block:
        @block.sync
        def _(eng):
            p.clear_last(eng, st)

        @block.vector
        def _(eng):
            for k in range(CT):
                g, b = VEC["gamma"][0] + k, VEC["beta"][0] + k
                eng.tensor_scalar(y[:, k, :], y[:, k, :], m.vec[:, g:g + 1], m.vec[:, b:b + 1], ALU.mult,
                                  ALU.add).then_inc(st.scaled, 1)
            for k in range(CT):
                eng.wait_ge(st.scaled, k + 1)
                eng.tensor_tensor(m.x[:, k, :], m.x[:, k, :], y[:, k, :], ALU.add).then_inc(st.added, 1)


def gates(p, m, g, st, u):
    nc, ps = p.nc, m.ps
    gw = m.vec[:, VEC["gate_w"][0]:VEC["gate_w"][1]].rearrange("p (k e) -> p k e", e=E)
    gb = m.vec[:, VEC["gate_b"][0]:VEC["gate_b"][1]]
    pr, rank, t1, t2 = g.probs, g.rank, g.t1, g.t2
    with nc.Block() as block:
        @block.sync
        def _(eng):
            p.clear_last(eng, st)

        @block.tensor
        def _(eng):
            for t in range(TT):
                for k in range(CT):
                    mm = eng.matmul(ps[:, 0, t * E:(t + 1) * E], u[:, k, t * P:(t + 1) * P], gw[:, k, :],
                                    start=k == 0, stop=k == CT - 1)
            mm.then_inc(st.scores, 1)

        @block.scalar
        def _(eng):
            for k in range(CT):
                eng.activation(g.u_hi[:, k, :], u[:, k, :], ACT.Copy).then_inc(st.high, 1)
            eng.wait_ge(st.step, 3)
            eng.activation(pr[:, :, :], pr[:, :, :], ACT.Exp).then_inc(st.exped, 1)

        @block.gpsimd
        def _(eng):
            for k in range(CT):
                eng.wait_ge(st.high, k + 1)
                eng.tensor_tensor(g.u_lo[:, k, :], u[:, k, :], g.u_hi[:, k, :].bitcast(F32), ALU.subtract).then_inc(st.low, 1)

        @block.vector
        def _(eng):
            n = [0]

            def then(ins):
                n[0] += 1
                ins.then_inc(st.step, 1)
                eng.wait_ge(st.step, n[0])

            def each(ap):
                return ap.unsqueeze(2).to_broadcast([P, TT, E])

            eng.wait_ge(st.scores, 1)
            then(eng.tensor_tensor(pr[:, :, :], ps[:, 0, 0:TT * E].rearrange("p (t e) -> p t e", e=E),
                                   gb.unsqueeze(1).to_broadcast([P, TT, E]), ALU.add))
            then(eng.tensor_reduce(t1[:, :], pr[:, :, :], AX.X, ALU.max))
            then(eng.tensor_tensor(pr[:, :, :], pr[:, :, :], each(t1[:, :]), ALU.subtract))
            eng.wait_ge(st.exped, 1)
            then(eng.tensor_reduce(t1[:, :], pr[:, :, :], AX.X, ALU.add))
            then(eng.reciprocal(t2[:, :], t1[:, :]))
            then(eng.tensor_tensor(pr[:, :, :], pr[:, :, :], each(t2[:, :]), ALU.mult))
            for e in range(E):
                first = True
                for o in range(E):
                    if o == e:
                        continue
                    dst = rank[:, :, e] if first else t1[:, :]
                    then(eng.tensor_tensor(dst, pr[:, :, o], pr[:, :, e], ALU.is_ge if o < e else ALU.is_gt))
                    if not first:
                        then(eng.tensor_tensor(rank[:, :, e], rank[:, :, e], t1[:, :], ALU.add))
                    first = False
            then(eng.tensor_scalar(rank[:, :, :], rank[:, :, :], 2.0, None, ALU.is_lt))
            then(eng.tensor_tensor(pr[:, :, :], pr[:, :, :], rank[:, :, :], ALU.mult))
            then(eng.tensor_reduce(t1[:, :], pr[:, :, :], AX.X, ALU.add))
            then(eng.tensor_scalar(t1[:, :], t1[:, :], 1e-9, None, ALU.add))
            then(eng.reciprocal(t2[:, :], t1[:, :]))
            then(eng.tensor_tensor(g.comb[:, :, :], pr[:, :, :], each(t2[:, :]), ALU.mult))


def experts(p, m, g, st, out):
    nc, ps, io = p.nc, m.ps, p.io
    SL = SLICE * P
    UNITS = SLICE * NH
    RING = 3

    def passes(eng, out_ap, w_hi, w_lo, x_hi, x_lo, start, stop):
        eng.matmul(out_ap, w_hi, x_hi, start=start, stop=False, skip_group_check=True)
        eng.matmul(out_ap, w_hi, x_lo, start=False, stop=False, skip_group_check=True)
        return eng.matmul(out_ap, w_lo, x_hi, start=False, stop=stop, skip_group_check=True)

    with nc.Block() as block:
        @block.sync
        def _(eng):
            p.clear_last(eng, st)

            def fetch(e, s, slot):
                eng.dma_start(g.raw1[:, slot, :, :], io["w1"][:, e, :, s * SL:(s + 1) * SL]).then_inc(st.got[slot], 16)
                eng.dma_start(g.raw2[:, slot, :, :], io["w2"][:, e, s * SLICE:(s + 1) * SLICE, :]).then_inc(st.got[slot], 16)

            for e in range(E):
                for s in range(SLICES):
                    i = e * SLICES + s
                    if i >= 2:
                        eng.wait_ge(st.split, 2 * (i - 1))
                    fetch(e, s, i % 2)
            eng.wait_ge(st.added, E * CT * NH)
            eng.dma_start(out, m.x[:, :, :]).then_inc(st.stored, 16)
            eng.wait_ge(st.stored, 16)

        @block.gpsimd
        def _(eng):
            for i in range(E * SLICES):
                slot = i % 2
                eng.wait_ge(st.high, 2 * i + 2)
                eng.wait_ge(st.got[slot], 32 * (i // 2 + 1))
                for raw, hi, lo in ((g.raw1, g.w1_hi, g.w1_lo), (g.raw2, g.w2_hi, g.w2_lo)):
                    if i >= 2:
                        eng.wait_ge(st.down, (i - 1) * UNITS)
                    eng.tensor_tensor(lo[:, slot, :, :], raw[:, slot, :, :], hi[:, slot, :, :].bitcast(F32),
                                      ALU.subtract).then_inc(st.split, 1)

        @block.scalar
        def _(eng):
            def gelu(i, v):
                e, s, u = i // SLICES, i % SLICES, i * UNITS + v
                t = s * SLICE + v // NH
                b = VEC["b1"][0] + e * HT + t
                eng.wait_ge(st.hidden, u + 1)
                if u >= RING:
                    eng.wait_ge(st.h_split, u - RING + 1)
                eng.activation(g.hid[:, u % RING, :], ps[:, 6 + u % 2, :], ACT.Gelu,
                               bias=m.vec[:, b:b + 1]).then_inc(st.gelu, 1)

            def high(i):
                slot = i % 2
                eng.wait_ge(st.got[slot], 32 * (i // 2 + 1))
                for raw, hi in ((g.raw1, g.w1_hi), (g.raw2, g.w2_hi)):
                    if i >= 2:
                        eng.wait_ge(st.down, (i - 1) * UNITS)
                        eng.wait_ge(st.split, 2 * (i - 1))
                    eng.activation(hi[:, slot, :, :], raw[:, slot, :, :], ACT.Copy).then_inc(st.high, 1)

            high(0)
            high(1)
            for i in range(E * SLICES):
                for v in range(UNITS):
                    gelu(i, v)
                    if v == 1 and 1 <= i < E * SLICES - 1:
                        high(i + 1)

        @block.vector
        def _(eng):
            def comb_rows(e, c):
                for t in range(HALF // P):
                    tile = c * (HALF // P) + t
                    eng.tensor_scalar(g.diag[:, tile, :], m.ident[:, :], g.comb[:, tile, e:e + 1], None,
                                      ALU.mult).then_inc(st.diag, 1)

            for e in range(E):
                for c in range(NH):
                    if e:
                        eng.wait_ge(st.rows, (e - 1) * NH + c + 1)
                    comb_rows(e, c)
                for c in range(NH):
                    eng.wait_ge(st.rows, e * NH + c + 1)
                    eng.tensor_copy(g.row[:, e, cols(c)], ps[:, 6 + c, :]).then_inc(st.row_taken, 1)
            for e in range(E):
                for u in range(e * SLICES * UNITS, (e + 1) * SLICES * UNITS):
                    eng.wait_ge(st.gelu, u + 1)
                    if u >= RING:
                        eng.wait_ge(st.down, u - RING + 1)
                    eng.tensor_copy(g.h_hi[:, u % RING, :], g.hid[:, u % RING, :]).then_inc(st.h_high, 1)
                    eng.wait_ge(st.h_high, u + 1)
                    eng.tensor_tensor(g.h_lo[:, u % RING, :], g.hid[:, u % RING, :],
                                      g.h_hi[:, u % RING, :].bitcast(F32), ALU.subtract).then_inc(st.h_split, 1)
                for c in range(NH):
                    eng.wait_ge(st.down, (e + 1) * SLICES * UNITS - (NH - 1 - c))
                    for f in range(CT):
                        b = VEC["b2"][0] + e * CT + f
                        if e:
                            eng.wait_ge(st.added, (e - 1) * CT * NH + c * CT + f + 1)
                        eng.wait_ge(st.row_taken, E * NH)
                        eng.scalar_tensor_tensor(out=g.tmp[:, c * CT + f, :], in0=ps[:, 2 * f + c, :],
                                                 scalar=m.vec[:, b:b + 1], in1=g.row[:, e, cols(c)], op0=ALU.add,
                                                 op1=ALU.mult).then_inc(st.weighed, 1)
                for c in range(NH):
                    for f in range(CT):
                        s = e * CT * NH + c * CT + f
                        eng.wait_ge(st.weighed, s + 1)
                        if e:
                            eng.wait_ge(st.added, s - CT * NH + 1)
                        eng.tensor_tensor(m.x[:, f, cols(c)], m.x[:, f, cols(c)], g.tmp[:, c * CT + f, :],
                                          ALU.add).then_inc(st.added, 1)

        @block.tensor
        def _(eng):
            def rows(e, c):
                if e:
                    eng.wait_ge(st.row_taken, (e - 1) * NH + c + 1)
                eng.wait_ge(st.diag, (e * NH + c + 1) * (HALF // P))
                for t in range(HALF // P):
                    mm = eng.matmul(ps[:, 6 + c, t * P:(t + 1) * P], g.ones[:, :], g.diag[:, c * (HALF // P) + t, :],
                                    start=True, stop=True)
                mm.then_inc(st.rows, 1)

            def up(i, v):
                slot, u = i % 2, i * UNITS + v
                t, c = v // NH, v % NH
                if v == 0:
                    eng.wait_ge(st.split, 2 * (i + 1))
                if u < 2:
                    eng.wait_ge(st.row_taken, (E - 1) * NH + u + 1)
                if u >= 2:
                    eng.wait_ge(st.gelu, u - 1)
                for k in range(CT):
                    w = slice(t * P, (t + 1) * P)
                    mm = passes(eng, ps[:, 6 + u % 2, :], g.w1_hi[:, slot, k, w], g.w1_lo[:, slot, k, w],
                                g.u_hi[:, k, cols(c)], g.u_lo[:, k, cols(c)], k == 0, k == CT - 1)
                mm.then_inc(st.hidden, 1)

            def down(i, v):
                e, s, slot, u = i // SLICES, i % SLICES, i % 2, i * UNITS + v
                t, c = v // NH, v % NH
                if e and s == 0 and v < NH:
                    eng.wait_ge(st.weighed, (e - 1) * CT * NH + (v + 1) * CT)
                eng.wait_ge(st.h_split, u + 1)
                for f in range(CT):
                    w = slice(f * P, (f + 1) * P)
                    mm = passes(eng, ps[:, 2 * f + c, :], g.w2_hi[:, slot, t, w], g.w2_lo[:, slot, t, w],
                                g.h_hi[:, u % RING, :], g.h_lo[:, u % RING, :], s == 0 and t == 0,
                                s == SLICES - 1 and t == SLICE - 1)
                mm.then_inc(st.down, 1)

            for e in range(E):
                for c in range(NH):
                    rows(e, c)
            units = [(i, v) for i in range(E * SLICES) for v in range(UNITS)]
            up(*units[0])
            up(*units[1])
            for n, (i, v) in enumerate(units):
                if n + 2 < len(units):
                    up(*units[n + 2])
                down(i, v)


def build(nc, io, out):
    with ExitStack() as ctx:
        p = Program(nc, io)
        banks = ctx.enter_context(nc.psum_tensor("banks", [P, 8, HALF], F32))
        resident = tensors(nc, ctx, [
                ("x", [P, CT, L], F32), ("vec", [P, VEC_N], F32), ("ident", [P, P], F32), ("mean_mat", [P, P], F32),
                ("pick", [P, BC], BF16), ("zeros", [P, HALF], BF16), ("eps5", [P, 1], F32), ("eps6", [P, 1], F32), ("Dsum", [P, CT], F32),
                ("kin", [P, CT, RANK], F32), ("kout", [P, C], F32), ("A0", [P, K0 * N * CT], F32),
                ("A1", [P, N * DT1], F32), ("w0x", [P, K0, CT, 96 + R0], F32), ("lowk", [P, K0 * C + DI], F32),
                ("proj1", [P, FT, RANK], F32), ("w_in", [P, CT, 2 * DI], F32), ("w1x", [P, DT1, 96 + R1], F32),
                ("w_out", [P, DT1, C], F32)])

        def stage(name, *signals):
            return semaphores(nc, ctx, name, *signals)

        s_load = stage("load", "small", "alog", "big", "own", "exped")
        ln = ("loaded0", "loaded1", "mean", "centred", "squared", "variance", "logged", "rstd", "normed")
        s_norm = [stage("norm_a", *ln), stage("norm_b", *ln)]
        s_turn = stage("turn", "turned")
        s_in = stage("inputs", "projected", "low", "dt", "absed", "exped", "logged", "split", "relued", "delta", "du")
        s_scan = stage("scan", "evacuated", "broadcast", "decay", "dbu", "scanned", "prod", "summed", "taken", "gated")
        s_gelu = stage("gelu", "gelu", "added")
        s_ffn = stage("ffn", "narrow", "z", "up", "gelu", "down", "g", "wide", "added")
        s_xz = stage("xz", "product", "tap", "silu_z", "silu_x")
        s_out = stage("out", "product", "copied")
        s_aff = stage("affine", "scaled", "added")
        s_gate = stage("gate", "scores", "high", "low", "step", "exped")
        s_moe = stage("moe", "got0", "got1", "high", "split", "hidden", "gelu", "h_high", "h_split", "down",
                      "diag", "rows", "row_taken", "weighed", "added", "stored")
        s_moe.got = [s_moe.got0, s_moe.got1]

        with ExitStack() as once:
            m = Named(ps=banks, **resident, **tensors(nc, once, [
                ("kmask", [P, CT, RANK], F32), ("emask", [P, C], F32), ("c2p", [P, C], F32)]))
            load_weights(p, m, s_load)
        with nc.Block() as block:
            @block.sync
            def _(eng):
                p.clear_last(eng, None)

        with nc.Fori(0, B) as b:
            x_in = io["x"][b]
            with ExitStack() as conv:
                m = Named(ps=banks, **resident, **tensors(nc, conv, [
                        ("dA", [P, CT, L], F32), ("dBu", [P, CT, L], F32), ("h", [P, CT, L], F32),
                        ("prod", [P, CT, L], F32), ("delta", [P, CT, L], F32), ("du", [P, CT, L], F32),
                        ("Bb", [P, 2, L], F32), ("Cb", [P, 2, L], F32), ("parts", [P, L], BF16), ("low", [P, L], F32),
                        ("big", [P, 4 * CT, L], F32)]))
                rstd = m.Cb[:, 0, :]
                u, ut, ys = m.big[:, 0:CT, :], m.big[:, CT:2 * CT, :], m.big[:, 2 * CT:3 * CT, :]

                layer_norm(p, m, s_norm[0], m.x, u, m.prod, rstd, m.eps6, load=x_in)
                turn_image(p, m, s_turn, u, ut)
                for n, k in enumerate((0, 2, 1, 3)):
                    src = ut if k % 2 else u
                    scan_inputs(p, m, s_in, lambda j: src[:, j, :], lambda t: m.w0x[:, k, t, :],
                                [src[:, t, :] for t in range(CT)], R0, k * C, VEC["dtb0"][0] + k * CT)

                    def take(eng, j, y):
                        if n == 0:
                            eng.scalar_tensor_tensor(out=ys[:, j, :], in0=u[:, j, :], scalar=m.Dsum[:, j:j + 1], in1=y,
                                                     op0=ALU.mult, op1=ALU.add).then_inc(s_scan.taken, 1)
                        elif k % 2 == 0:
                            eng.tensor_tensor(ys[:, j, :], ys[:, j, :], y, ALU.add).then_inc(s_scan.taken, 1)
                        else:
                            v = ys[:, j, :].rearrange("p (h w) -> p h w", w=WW)
                            eng.tensor_tensor(v, v, y.rearrange("p (w h) -> p h w", w=WW), ALU.add).then_inc(s_scan.taken, 1)

                    selective_scan(p, m, s_scan, m.A0, k * N * CT, k >= 2, take)
                layer_norm(p, m, s_norm[0], ys, ys, m.prod, rstd, m.eps5)
                gated_residual(p, m, s_gelu, ys)
                layer_norm(p, m, s_norm[0], m.x, m.h, m.prod, rstd, m.eps5)
                kron_ffn(p, m, s_ffn, m.h)

                xin, z = m.big[:, 0:DT1, :], m.big[:, DT1:2 * DT1, :]
                layer_norm(p, m, s_norm[0], m.x, m.h, m.prod, rstd, m.eps6)
                in_projection(p, m, s_xz, m.h, xin, z)
                for half in range(GROUPS1):
                    t0 = half * CT
                    scan_inputs(p, m, s_in, lambda j: xin[:, t0 + j, :], lambda t: m.w1x[:, t, :],
                                [xin[:, t, :] for t in range(DT1)], R1, K0 * C + t0 * P, VEC["dtb1"][0] + t0,
                                project=half == 0)

                    def gate(eng, j, y):
                        d = VEC["D1"][0] + t0 + j
                        eng.scalar_tensor_tensor(out=m.h[:, j, :], in0=xin[:, t0 + j, :], scalar=m.vec[:, d:d + 1], in1=y,
                                                 op0=ALU.mult, op1=ALU.add).then_inc(s_scan.taken, 1)
                        if j:
                            gate_with(eng, j - 1)
                        if j == CT - 1:
                            gate_with(eng, j)

                    def gate_with(eng, j):
                        eng.wait_ge(s_scan.taken, j + 1)
                        eng.tensor_tensor(z[:, t0 + j, :], z[:, t0 + j, :], m.h[:, j, :], ALU.mult).then_inc(s_scan.gated, 1)

                    selective_scan(p, m, s_scan, m.A1, half * N * CT, False, gate)
                out_projection(p, m, s_out, z, m.h)
                layer_norm(p, m, s_norm[0], m.h, m.h, m.prod, rstd, m.eps5)
                affine_residual(p, m, s_aff, m.h)

            with ExitStack() as moe:
                SL = SLICE * P
                m = Named(ps=banks, **resident)
                g = Named(**tensors(nc, moe, [
                        ("un", [P, CT, L], F32),
                        ("u_hi", [P, CT, L], F32R), ("u_lo", [P, CT, L], F32R),
                        ("raw1", [P, 2, CT, SL], F32), ("raw2", [P, 2, SLICE, C], F32),
                        ("w1_hi", [P, 2, CT, SL], F32R), ("w1_lo", [P, 2, CT, SL], F32R),
                        ("w2_hi", [P, 2, SLICE, C], F32R), ("w2_lo", [P, 2, SLICE, C], F32R),
                        ("hid", [P, 3, HALF], F32), ("h_hi", [P, 3, HALF], F32R), ("h_lo", [P, 3, HALF], F32R),
                        ("row", [P, E, L], F32), ("tmp", [P, CT * NH, HALF], F32), ("diag", [P, TT, P], F32),
                        ("ones", [P, P], F32), ("probs", [P, TT, E], F32), ("rank", [P, TT, E], F32),
                        ("comb", [P, TT, E], F32), ("t1", [P, TT], F32), ("t2", [P, TT], F32)]))
                layer_norm(p, m, s_norm[1], m.x, g.un, g.tmp[:, :, :].rearrange("p (k c) n -> p k (c n)", c=NH), g.row[:, 0, :], m.eps5)
                with nc.Block() as block:
                    @block.sync
                    def _(eng):
                        p.clear_last(eng, None)

                    @block.vector
                    def _(eng):
                        eng.memset(g.ones[:, :], 1.0)
                gates(p, m, g, s_gate, g.un)
                experts(p, m, g, s_moe, out[b])
            with nc.Block() as block:
                @block.sync
                def _(eng):
                    p.clear_last(eng, None)


def kernel(**inputs):
    import concourse.bacc as bacc
    import ml_dtypes
    from concourse.bass_utils import run_bass_kernel_spmd

    a = {k: np.asarray(v) for k, v in inputs.items()}

    def rows(v, t):
        return v.reshape(t, P, *v.shape[1:]).swapaxes(0, 1)

    wx0 = a["L0_conv_x_proj_weight"]
    bc = wx0[:, R0:]
    wx0 = np.concatenate([bc, bc, bc, wx0[:, :R0]], axis=1).transpose(2, 0, 1)
    wx1 = a["L1_conv_x_proj_w"]
    bc = wx1[R1:]
    wx1 = np.concatenate([bc, bc, bc, wx1[:R1]], axis=0).T
    vec = {
        "dtb0": a["L0_conv_dt_projs_bias"].reshape(K0 * CT, P).T, "D0": a["L0_conv_Ds"].reshape(K0 * CT, P).T,
        "dtb1": a["L1_conv_dt_proj_b"].reshape(DT1, P).T, "D1": a["L1_conv_D"].reshape(DT1, P).T,
        "conv_w": rows(a["L1_conv_conv_w"], DT1).reshape(P, -1), "conv_b": a["L1_conv_conv_b"].reshape(DT1, P).T,
        "ln_w": a["L0_conv_ln_weight"].reshape(CT, P).T, "ln_b": a["L0_conv_ln_bias"].reshape(CT, P).T,
        "gamma": a["L1_conv_ln_gamma"].reshape(CT, P).T, "beta": a["L1_conv_ln_beta"].reshape(CT, P).T,
        "c2": np.tile(a["L0_ffn_c_fc_2"][0], RANK).reshape(CT, P).T,
        "gate_b": np.tile(a["L1_ffn_gate_b"][None], (P, 1)),
        "b1": a["L1_ffn_b1"].reshape(E * HT, P).T, "b2": a["L1_ffn_b2"].reshape(E * CT, P).T,
        "gate_w": rows(a["L1_ffn_gate_w"], CT).reshape(P, -1),
    }
    block = np.arange(C)[:, None] // KR == np.arange(RANK)[None]
    arrays = {
        "x": a["x"].reshape(B, CT, P, L).transpose(0, 2, 1, 3),
        "ident": np.eye(P, dtype=np.float32),
        "mean_mat": np.full((P, P), 1.0 / C, np.float32),
        "pick": (np.arange(P)[:, None] % BC == np.arange(BC)[None]).astype(ml_dtypes.bfloat16),
        "vec": np.concatenate([vec[n] for n in VEC], axis=1),
        "kmask": rows(block.astype(np.float32), CT), "emask": block.T.astype(np.float32),
        "c2p": np.tile(a["L0_ffn_c_proj_2"][:, 0], (RANK, RANK)),
        "A0": a["L0_conv_A_logs"].reshape(K0, CT, P, N).transpose(2, 0, 3, 1).reshape(P, -1),
        "A1": a["L1_conv_A_log"].reshape(GROUPS1, CT, P, N).transpose(2, 0, 3, 1).reshape(P, -1),
        "w0x": wx0.reshape(CT, P, K0, 96 + R0).transpose(1, 2, 0, 3),
        "dtw0": a["L0_conv_dt_projs_weight"].transpose(2, 0, 1).reshape(R0, K0 * C),
        "dtw1": a["L1_conv_dt_proj_w"].T, "fc1": a["L0_ffn_c_fc_1"].T,
        "proj1": rows(a["L0_ffn_c_proj_1"].T, FT),
        "w_in": rows(a["L1_conv_in_proj_w"].T, CT), "w1x": rows(wx1, DT1),
        "w_out": rows(a["L1_conv_out_proj_w"].T, DT1),
        "w1": a["L1_ffn_w1"].reshape(E, CT, P, HID).transpose(2, 0, 1, 3),
        "w2": a["L1_ffn_w2"].reshape(E, HT, P, C).transpose(2, 0, 1, 3),
    }
    arrays = {f"{n}_in": np.ascontiguousarray(v) for n, v in arrays.items()}
    nc = bacc.Bacc("TRN2", target_bir_lowering=False, num_devices=1)
    io = {n[:-3]: nc.dram_tensor(n, v.shape, mybir.dt.from_np(v.dtype), kind="ExternalInput").ap()
          for n, v in arrays.items()}
    out = nc.dram_tensor("out", (B, P, CT, L), F32, kind="ExternalOutput").ap()
    build(nc, io, out)
    r = run_bass_kernel_spmd(nc, [arrays], core_ids=[0])
    y = r.results[0]["out"]
    return y.transpose(0, 2, 1, 3).reshape(B, C, HH, WW)
```

```python
from contextlib import ExitStack

import numpy as np

import concourse.bass as bass
import concourse.mybir as mybir

ALU = mybir.AluOpType
ACT = mybir.ActivationFunctionType
AX = mybir.AxisListType
F32 = mybir.dt.float32
F32R = mybir.dt.float32r
BF16 = mybir.dt.bfloat16

EXP_LN = "natural_log_exp_and_others"

P = 128
B, C, HH, WW = 4, 384, 32, 32
L = HH * WW
CT = C // P
HALF = 512
NH = L // HALF
N = 16
K0, R0 = 4, 12
DI, R1 = 768, 24
DT1 = DI // P
GROUPS1 = DT1 // CT
BC = 2 * N
TAPS = 4
FF, RANK = 1536, 32
FT = FF // P
KR = C // RANK
E, HID = 4, 1536
HT = HID // P
SLICE = 3
SLICES = HT // SLICE
TT = L // P

VEC = {}
_at = 0
for _name, _n in [("D0", K0 * CT), ("D1", DT1), ("conv_w", DT1 * TAPS),
                  ("conv_b", DT1), ("ln_w", CT), ("ln_b", CT), ("gamma", CT), ("beta", CT), ("c2", CT),
                  ("gate_b", E), ("b1", E * HT), ("b2", E * CT), ("gate_w", CT * E)]:
    VEC[_name] = (_at, _at + _n)
    _at += _n
VEC_N = _at


def cols(c):
    return slice(c * HALF, (c + 1) * HALF)


def over_tiles(ap, n=CT):
    return ap.unsqueeze(1).to_broadcast([ap.shape[0], n, ap.shape[1]])


class Named(dict):

    __getattr__ = dict.__getitem__


def tensors(nc, stack, table):
    return {name: stack.enter_context(nc.sbuf_tensor(name, shape, dt)) for name, shape, dt in table}


def semaphores(nc, stack, stage, *signals):
    named = {s: stack.enter_context(nc.semaphore(f"{stage}_{s}")) for s in signals}
    return Named(all=list(named.values()), **named)


class Program:
    def __init__(self, nc, io):
        self.nc, self.io = nc, io
        self.last = None

    def clear_last(self, eng, stage):
        if self.last is not None:
            for s in self.last.all:
                eng.sem_clear(s)
        self.last = stage


def load_half(eng, m, image, x, c):
    eng.dma_start(m.x[:, :, cols(c)], x[:, :, cols(c)]).then_inc(image.loaded[c], 16)


def load_weights(p, m, st, image):
    nc, io = p.nc, p.io
    with nc.Block() as block:
        @block.sync
        def _(eng):
            eng.dma_start(m.ident[:, :], io["ident"]).then_inc(st.small, 16)
            eng.dma_start(m.mean_mat[:, :], io["mean_mat"]).then_inc(st.small, 16)
            eng.dma_start(m.pick[:, :], io["pick"]).then_inc(st.small, 16)
            eng.dma_start(m.vec[:, :], io["vec"]).then_inc(st.small, 16)
            eng.dma_start(m.kmask[:, :, :], io["kmask"]).then_inc(st.small, 16)
            eng.dma_start(m.emask[0:2 * RANK, :], io["emask"]).then_inc(st.small, 16)
            eng.dma_start(m.c2p[0:2 * RANK, :], io["c2p"]).then_inc(st.small, 16)
            eng.dma_start(m.A0[:, :], io["A0"]).then_inc(st.alog, 16)
            eng.dma_start(m.A1[:, :], io["A1"]).then_inc(st.alog, 16)
            eng.dma_start(m.w0x[:, :, :, :], io["w0x"]).then_inc(st.big, 16)
            eng.dma_start(m.lowk[96:97 + R0, 0:K0 * C], io["dtw0"]).then_inc(st.big, 16)
            eng.dma_start(m.lowk[96:97 + R1, K0 * C:K0 * C + DI], io["dtw1"]).then_inc(st.big, 16)
            eng.dma_start(m.fc2[:, :, :], io["proj1"]).then_inc(st.kron, 16)
            eng.dma_start(m.w1x[:, :, :], io["w1x"]).then_inc(st.big, 16)
            for c in range(NH):
                load_half(eng, m, image, io["x"][0], c)
            eng.sem_inc(image.stored, 16 * NH)
            eng.wait_ge(st.big, 16 * 4)
            p.clear_last(eng, st)

        @block.vector
        def _(eng):
            eng.memset(m.eps5[:, :], 1e-5).then_inc(st.own, 1)
            eng.memset(m.eps6[:, :], 1e-6).then_inc(st.own, 1)
            eng.wait_ge(st.small, 16 * 7)
            for kt in range(CT):
                a = VEC["c2"][0] + kt
                eng.tensor_scalar(m.kin[:, kt, :], m.kmask[:, kt, :], m.vec[:, a:a + 1], None,
                                  ALU.mult).then_inc(st.own, 1)
            eng.tensor_tensor(m.kout[0:2 * RANK, :], m.emask[0:2 * RANK, :], m.c2p[0:2 * RANK, :],
                              ALU.mult).then_inc(st.own, 1)
            eng.wait_ge(st.kron, 16)
            eng.tensor_copy(m.proj1[:, :, 0:RANK], m.fc2[:, :, :]).then_inc(st.split, 1)
            eng.wait_ge(st.split, 1)
            eng.tensor_tensor(m.proj1[:, :, RANK:2 * RANK], m.fc2[:, :, :], m.proj1[:, :, 0:RANK].bitcast(F32),
                              ALU.subtract).then_inc(st.own, 1)
            eng.wait_ge(st.exped, 2)
            eng.tensor_scalar(m.A0[:, :], m.A0[:, :], -1.0, None, ALU.mult).then_inc(st.own, 1)
            eng.tensor_scalar(m.A1[:, :], m.A1[:, :], -1.0, None, ALU.mult).then_inc(st.own, 1)
            d = m.vec[:, VEC["D0"][0]:VEC["D0"][1]].rearrange("p (k t) -> p t k", t=CT)
            eng.tensor_reduce(m.Dsum[:, :], d, AX.X, ALU.add).then_inc(st.own, 1)

        @block.scalar
        def _(eng):
            eng.wait_ge(st.alog, 32)
            eng.activation(m.A0[:, :], m.A0[:, :], ACT.Exp).then_inc(st.exped, 1)
            eng.activation(m.A1[:, :], m.A1[:, :], ACT.Exp).then_inc(st.exped, 1)


def layer_norm(p, m, st, src, dst, sq, rstd, eps, loaded=None, fetch=None, aside=None, after=None):
    nc, ps = p.nc, m.ps
    with nc.Block() as block:
        @block.sync
        def _(eng):
            p.clear_last(eng, st)
            if fetch is not None:
                fetch(eng)

        @block.gpsimd
        def _(eng):
            if aside is not None:
                aside(eng)

        @block.tensor
        def _(eng):
            for c in range(NH):
                if loaded is not None:
                    eng.wait_ge(loaded[c], 16)
                for k in range(CT):
                    mm = eng.matmul(ps[:, c, :], m.mean_mat[:, :], src[:, k, cols(c)], start=k == 0, stop=k == CT - 1)
                mm.then_inc(st.mean, 1)
            for c in range(NH):
                for k in range(CT):
                    eng.wait_ge(st.squared, c * CT + k + 1)
                    mm = eng.matmul(ps[:, 2 + c, :], m.mean_mat[:, :], sq[:, k, cols(c)], start=k == 0, stop=k == CT - 1)
                mm.then_inc(st.variance, 1)
            if after is not None:
                eng.wait_ge(st.normed, 1)
                after(eng)

        @block.vector
        def _(eng):
            for c in range(NH):
                eng.wait_ge(st.mean, c + 1)
                for k in range(CT):
                    eng.tensor_tensor(dst[:, k, cols(c)], src[:, k, cols(c)], ps[:, c, :],
                                      ALU.subtract).then_inc(st.centred, 1)
            for c in range(NH):
                eng.wait_ge(st.rstd, c + 1)
                eng.wait_ge(st.centred, (c + 1) * CT)
                eng.tensor_tensor(dst[:, :, cols(c)], dst[:, :, cols(c)], over_tiles(rstd[:, cols(c)]),
                                  ALU.mult).then_inc(st.normed, 1)

        @block.scalar
        def _(eng):
            eng.preload_act_table_set(EXP_LN)
            for c in range(NH):
                for k in range(CT):
                    eng.wait_ge(st.centred, c * CT + k + 1)
                    eng.activation(sq[:, k, cols(c)], dst[:, k, cols(c)], ACT.Square).then_inc(st.squared, 1)
            for c in range(NH):
                eng.wait_ge(st.variance, c + 1)
                eng.activation(rstd[:, cols(c)], ps[:, 2 + c, :], ACT.Ln, bias=eps[:, :]).then_inc(st.logged, 1)
                eng.wait_ge(st.logged, c + 1)
                eng.activation(rstd[:, cols(c)], rstd[:, cols(c)], ACT.Exp, scale=-0.5).then_inc(st.rstd, 1)


def selective_scans(p, m, st, phases, load_ahead=None, turned=None):
    nc, ps, low = p.nc, m.ps, m.low
    PAIRS = N // 2
    STEPS = N * CT
    SCAN0, EVAC0, PROD0, DBU0, SUM0 = 3, 1, 6, 6, 3
    PROJECT_TURNS, DT_TURNS = (8, 9), (10, 12, 13)
    AHEAD_PAIR = (PROJECT_TURNS[0] - 2) // 2
    EXPS, LOGS = [(11, 2), (13, 2), (14, 2)], [(12, 1), (14, 1), (15, 1)]
    CAPS, DELTAS = DT_TURNS, (12, 13, 14)
    last_ph = len(phases) - 1
    made = [sum(x.project for x in phases[:i + 1]) for i in range(len(phases))]

    def y_banks(j):
        return ps[:, 2 * j + 2:2 * j + 4, :]

    def dt_bank(ph, j):
        return 2 * j if ph == 0 else 0

    def halves(ap):
        return ap.rearrange("p (c n) -> p c n", c=NH)

    def parts(ph):
        return m.parts[:, (made[ph] - 1) % 2, :]

    def fresh(ph):
        return ph <= last_ph and phases[ph].project

    def row(ph, n):
        if n < N:
            return ph, n
        return (ph + 1, n - N) if ph < last_ph else None

    with nc.Block() as block:
        @block.sync
        def _(eng):
            p.clear_last(eng, st)
            if load_ahead is not None:
                eng.wait_ge(st.scanned, SCAN0 + STEPS)
                load_ahead(eng, st.loaded)
                eng.wait_ge(st.loaded, 16)

        @block.tensor
        def _(eng):
            eng.sem_inc(st.summed, SUM0)

            def project(ph, c):
                x = phases[ph]
                if ph == 2 and turned is not None:
                    eng.wait_ge(st.turned, CT)
                for k, src in enumerate(x.kts):
                    mm = eng.matmul(ps[0:96 + x.rank, c, :], x.wx(k), src[:, cols(c)],
                                    start=k == 0, stop=k == len(x.kts) - 1)
                mm.then_inc(st.projected, 1)

            def dt_product(ph, j):
                x, bank = phases[ph], dt_bank(ph, j)
                eng.wait_ge(st.low, made[ph] * NH)
                a = x.dt_at + j * P
                for c in range(NH):
                    mm = eng.matmul(ps[:, bank + c, :], m.lowk[96:97 + x.rank, a:a + P],
                                    low[96:97 + x.rank, cols(c)], start=True, stop=True)
                mm.then_inc(st.dt, 1)

            def broadcast(ph, q, i, r):
                eng.wait_ge(st.evacuated, q * 4 + (ph * 2 * N + 2 * i + r + EVAC0))
                at = r * N + q * 2 + i
                lhs = m.pick[0:96, at:at + 1] if isinstance(at, int) else m.pick[0:96, bass.ds(at, 1)]
                for c in range(NH):
                    mm = eng.matmul(ps[:, c, :], lhs.to_broadcast([96, P]), parts(ph)[0:96, cols(c)],
                                    start=True, stop=True)
                mm.then_inc(st.broadcast, 1)

            def broadcast_row(at, r):
                if at is not None:
                    ph, n = at
                    if n == 0 and r == 0 and fresh(ph):
                        eng.wait_ge(st.parts, made[ph])
                    broadcast(ph, n // 2, n % 2, r)

            def add(ph, q, i, j, first=False, last=False):
                eng.wait_ge(st.prod, q * 6 + (ph * STEPS + 3 * i + j + 1 + PROD0))
                if first and ph:
                    eng.wait_ge(st.taken, (ph - 1) * CT + j + 1)
                elif first and j + 1 < CT:
                    eng.wait_ge(st.got_dt, j + 2)
                for c in range(NH):
                    mm = eng.matmul(ps[:, 2 * j + 2 + c, :], m.ident[:, :], m.prod[:, j, cols(c)],
                                    start=first, stop=last, skip_group_check=True)
                mm.then_inc(st.summed, 1)

            def turn(ph, q, i):
                broadcast(ph, q + 1, i, 0)
                add(ph, q, i, 0)
                add(ph, q, i, 1)
                broadcast(ph, q + 1, i, 1)
                add(ph, q, i, 2)

            def turn_out(ph, n):
                q, i = n // 2, n % 2
                ahead = row(ph, n + 2)
                at = dict(first=n == 0, last=n == N - 1)
                if (n + 1 in PROJECT_TURNS and fresh(ph + 1)) or (n + 1 in DT_TURNS and ph < last_ph):
                    eng.wait_ge(st.evacuated, ph * 2 * N + 2 * (n + 2) + EVAC0)
                    if n + 1 in PROJECT_TURNS:
                        c = PROJECT_TURNS.index(n + 1)
                        project(ph + 1, c)
                        add(ph, q, i, 0, **at)
                        eng.wait_ge(st.low, (made[ph + 1] - 1) * NH + c + 1)
                    else:
                        j = DT_TURNS.index(n + 1)
                        dt_product(ph + 1, j)
                        add(ph, q, i, 0, **at)
                        eng.wait_ge(st.got_dt, (ph + 1) * CT + j + 1)
                    broadcast_row(ahead, 0)
                    add(ph, q, i, 1, **at)
                    broadcast_row(ahead, 1)
                    add(ph, q, i, 2, **at)
                else:
                    broadcast_row(ahead, 0)
                    add(ph, q, i, 0, **at)
                    add(ph, q, i, 1, **at)
                    broadcast_row(ahead, 1)
                    add(ph, q, i, 2, **at)

            for c in range(NH):
                project(0, c)
            for j in range(CT):
                dt_product(0, j)
            eng.wait_ge(st.got_dt, 1)
            broadcast_row((0, 0), 0)
            broadcast_row((0, 0), 1)
            broadcast_row((0, 1), 0)
            broadcast_row((0, 1), 1)
            for ph in range(len(phases)):
                turn_out(ph, 0)
                turn_out(ph, 1)
                with eng.Fori(1, AHEAD_PAIR) as q:
                    turn(ph, q, 0)
                    turn(ph, q, 1)
                for n in range(2 * AHEAD_PAIR, N):
                    turn_out(ph, n)

        @block.scalar
        def _(eng):
            eng.preload_act_table_set(EXP_LN)
            eng.sem_inc(st.evacuated, EVAC0)

            def read_dt(ph, j):
                bank = dt_bank(ph, j)
                eng.wait_ge(st.dt, ph * CT + j + 1)
                eng.activation(halves(m.du[:, ph % 2, j, :]), ps[:, bank:bank + NH, :], ACT.Copy).then_inc(st.got_dt, 1)

            def exp_dt(ph, j):
                d = m.delta[:, ph % 2, j, :]
                eng.wait_ge(st.capped, ph * CT + j + 1)
                eng.activation(d, d, ACT.Exp).then_inc(st.exped, 1)

            def log_dt(ph, j):
                d = m.delta[:, ph % 2, j, :]
                eng.wait_ge(st.exped, ph * CT + j + 1)
                eng.activation(d, d, ACT.Ln, bias=1.0).then_inc(st.logged, 1)

            def evacuate(ph, q, i, r):
                ring, used, first = ((m.Bb, st.dbu, DBU0), (m.Cb, st.prod, PROD0))[r]
                eng.wait_ge(st.broadcast, q * 4 + (ph * 2 * N + 2 * i + r + 1))
                eng.wait_ge(used, q * 6 + (ph * STEPS + 3 * i + first - 3))
                eng.activation(halves(ring[:, i, :]), ps[:, 0:NH, :], ACT.Copy).then_inc(st.evacuated, 1)

            def evacuate_row(at, r):
                if at is not None:
                    ph, n = at
                    evacuate(ph, n // 2, n % 2, r)

            def decay(ph, q, i, j):
                eng.wait_ge(st.scanned, q * 6 + (ph * STEPS + 3 * i + j + 1))
                at = phases[ph].a_at + (q * 2 + i) * CT + j
                A = phases[ph].A
                scale = A[:, at:at + 1] if isinstance(at, int) else A[:, bass.ds(at, 1)]
                eng.activation(m.dA[:, j, :], m.delta[:, ph % 2, j, :], ACT.Exp, scale=scale).then_inc(st.decay, 1)

            def turn(ph, q, i):
                decay(ph, q, i, 0)
                evacuate(ph, q + i, 1 - i, 0)
                decay(ph, q, i, 1)
                decay(ph, q, i, 2)
                evacuate(ph, q + i, 1 - i, 1)

            def take_projection(ph, c):
                x, k = phases[ph], made[ph] - 1
                eng.wait_ge(st.projected, k * NH + c + 1)
                if ph == 0:
                    eng.wait_ge(st.ones, 1)
                eng.activation(low[0:96 + x.rank, cols(c)], ps[0:96 + x.rank, c, :], ACT.Copy).then_inc(st.low, 1)

            def first_parts(ph):
                eng.wait_ge(st.low, made[ph] * NH)
                eng.activation(parts(ph)[0:96, :], low[0:96, :], ACT.Copy).then_inc(st.first, 1)

            def second_parts(ph):
                eng.wait_ge(st.left, made[ph])
                eng.activation(parts(ph)[0:64, :], low[0:64, :], ACT.Copy).then_inc(st.second, 1)

            def third_parts(ph):
                eng.wait_ge(st.third, made[ph])
                eng.activation(parts(ph)[0:32, :], low[0:32, :], ACT.Copy).then_inc(st.parts, 1)

            def ahead(ph, at):
                if at[1] == 0 and at[0] in DT_TURNS:
                    read_dt(ph, DT_TURNS.index(at[0]))
                if fresh(ph):
                    if at[1] == 0 and at[0] in PROJECT_TURNS:
                        take_projection(ph, PROJECT_TURNS.index(at[0]))
                    if at == (9, 2):
                        first_parts(ph)
                    if at == (11, 1):
                        second_parts(ph)
                    if at == (13, 1):
                        third_parts(ph)
                if at in EXPS:
                    exp_dt(ph, EXPS.index(at))
                if at in LOGS:
                    log_dt(ph, LOGS.index(at))

            def turn_out(ph, n):
                q, i = n // 2, n % 2
                following = row(ph, n + 1)
                decay(ph, q, i, 0)
                if ph < last_ph:
                    ahead(ph + 1, (n, 0))
                decay(ph, q, i, 1)
                evacuate_row(following, 0)
                if ph < last_ph:
                    ahead(ph + 1, (n, 1))
                decay(ph, q, i, 2)
                evacuate_row(following, 1)
                if ph < last_ph:
                    ahead(ph + 1, (n, 2))

            for c in range(NH):
                take_projection(0, c)
            first_parts(0)
            read_dt(0, 0)
            exp_dt(0, 0)
            second_parts(0)
            read_dt(0, 1)
            log_dt(0, 0)
            exp_dt(0, 1)
            third_parts(0)
            evacuate_row((0, 0), 0)
            read_dt(0, 2)
            log_dt(0, 1)
            exp_dt(0, 2)
            evacuate_row((0, 0), 1)
            log_dt(0, 2)
            for ph in range(len(phases)):
                for j in range(CT):
                    eng.wait_ge(st.delta, ph * CT + j + 1)
                    decay(ph, 0, 0, j)
                    if j == 0:
                        evacuate(ph, 0, 1, 0)
                evacuate(ph, 0, 1, 1)
                turn(ph, 0, 1)
                with eng.Fori(1, AHEAD_PAIR) as q:
                    turn(ph, q, 0)
                    turn(ph, q, 1)
                for n in range(2 * AHEAD_PAIR, N):
                    turn_out(ph, n)

        @block.gpsimd
        def _(eng):
            eng.memset(low[96:128, :], 1.0).then_inc(st.ones, 1)
            eng.sem_inc(st.dbu, DBU0)

            def drive(ph, q, i, fresh_du=False):
                eng.wait_ge(st.evacuated, q * 4 + (ph * 2 * N + 2 * i + 1 + EVAC0))
                for j in range(CT):
                    if fresh_du:
                        du(ph, j)
                        eng.wait_ge(st.du, ph * CT + j + 1)
                    eng.wait_ge(st.scanned, q * 6 + (ph * STEPS + 3 * i + j + 1))
                    eng.tensor_tensor(m.dBu[:, j, :], m.du[:, ph % 2, j, :], m.Bb[:, i, :], ALU.mult).then_inc(st.dbu, 1)

            def du(ph, j):
                eng.wait_ge(st.delta, ph * CT + j + 1)
                eng.tensor_tensor(m.du[:, ph % 2, j, :], m.delta[:, ph % 2, j, :], phases[ph].u(j),
                                  ALU.mult).then_inc(st.du, 1)

            if turned is not None:
                u, ut = turned
                eng.wait_ge(st.ones, 1)
                for k in range(CT):
                    if k:
                        eng.wait_ge(st.turned, k)
                    eng.tensor_copy(ut[:, k, :].rearrange("p (w h) -> p w h", w=WW),
                                    u[:, k, :].rearrange("p (h w) -> p w h", w=WW)).then_inc(st.turned, 1)
                eng.wait_ge(st.turned, CT)
            for ph in range(len(phases)):
                if ph:
                    eng.wait_ge(st.du, (ph + 1) * CT)
                drive(ph, 0, 0, fresh_du=ph == 0)
                drive(ph, 0, 1)
                with eng.Fori(1, PAIRS - 2) as q:
                    drive(ph, q, 0)
                    drive(ph, q, 1)
                for n in range(N - 4, N):
                    drive(ph, n // 2, n % 2)
                    if ph < last_ph and n >= N - CT:
                        du(ph + 1, n - (N - CT))

        @block.vector
        def _(eng):
            eng.sem_inc(st.scanned, SCAN0)
            eng.sem_inc(st.prod, PROD0)

            def leave_first(ph):
                eng.wait_ge(st.first, made[ph])
                eng.tensor_tensor(low[0:96, :], low[0:96, :], parts(ph)[0:96, :], ALU.subtract).then_inc(st.left, 1)

            def leave_second(ph):
                eng.wait_ge(st.second, made[ph])
                eng.tensor_tensor(low[0:32, :], low[0:32, :], parts(ph)[0:32, :], ALU.subtract).then_inc(st.third, 1)

            def cap(ph, j):
                eng.wait_ge(st.got_dt, ph * CT + j + 1)
                eng.tensor_scalar(m.delta[:, ph % 2, j, :], m.du[:, ph % 2, j, :], 30.0, None, ALU.min).then_inc(st.capped, 1)

            def delta(ph, j):
                slot = ph % 2
                eng.wait_ge(st.logged, ph * CT + j + 1)
                eng.scalar_tensor_tensor(out=m.delta[:, slot, j, :], in0=m.delta[:, slot, j, :], scalar=30.0,
                                         in1=m.du[:, slot, j, :], op0=ALU.min, op1=ALU.max).then_inc(st.delta, 1)

            def scan(ph, q, s):
                j = s % CT
                flip = (lambda ap: ap[:, ::-1]) if phases[ph].reverse else (lambda ap: ap)
                eng.wait_ge(st.decay, q * 6 + (ph * STEPS + s + 1))
                eng.wait_ge(st.dbu, q * 6 + (ph * STEPS + s + 1 + DBU0))
                eng.wait_ge(st.prod, q * 6 + (ph * STEPS + s - 3 + 1 + PROD0))
                eng.tensor_tensor_scan(flip(m.h[:, j, :]), flip(m.dA[:, j, :]), flip(m.dBu[:, j, :]), 0.0,
                                       ALU.mult, ALU.add).then_inc(st.scanned, 1)

            def weigh(ph, q, s):
                j = s % CT
                if j == 0:
                    eng.wait_ge(st.evacuated, q * 4 + (ph * 2 * N + 2 * (s // CT) + 2 + EVAC0))
                eng.wait_ge(st.scanned, q * 6 + (ph * STEPS + s + 1 + SCAN0))
                eng.wait_ge(st.summed, q * 6 + (ph * STEPS + s + 1))
                eng.tensor_tensor(m.prod[:, j, :], m.h[:, j, :], m.Cb[:, s // CT, :], ALU.mult).then_inc(st.prod, 1)

            def take(ph, j):
                eng.wait_ge(st.summed, SUM0 + (ph + 1) * STEPS - CT + j + 1)
                if phases[ph].after:
                    eng.wait_ge(st.taken, (ph - 1) * CT + j + 1)
                phases[ph].take(eng, j, y_banks(j).rearrange("p c n -> p (c n)"))

            def pair(ph, q):
                scan(ph, q, 0)
                for s in range(1, 2 * CT):
                    scan(ph, q, s)
                    weigh(ph, q, s - 1)
                weigh(ph, q, 2 * CT - 1)

            def pair_out(ph, q):
                for s in range(2 * CT):
                    scan(ph, q, s)
                    if s:
                        weigh(ph, q, s - 1)
                    if q == 0 and ph and 1 <= s <= CT:
                        take(ph - 1, s - 1)
                    if s == CT:
                        between(ph, 2 * q)
                weigh(ph, q, 2 * CT - 1)
                between(ph, 2 * q + 1)

            def between(ph, n):
                if ph < last_ph:
                    if fresh(ph + 1) and n == 9:
                        leave_first(ph + 1)
                    if fresh(ph + 1) and n == 11:
                        leave_second(ph + 1)
                    if n in CAPS:
                        cap(ph + 1, CAPS.index(n))
                    if n in DELTAS:
                        delta(ph + 1, DELTAS.index(n))

            leave_first(0)
            cap(0, 0)
            leave_second(0)
            cap(0, 1)
            delta(0, 0)
            cap(0, 2)
            delta(0, 1)
            delta(0, 2)
            for ph in range(len(phases)):
                pair_out(ph, 0)
                with eng.Fori(1, AHEAD_PAIR + 1) as q:
                    pair(ph, q)
                for q in range(AHEAD_PAIR + 1, PAIRS):
                    pair_out(ph, q)
            for j in range(CT):
                take(last_ph, j)


def gated_residual(p, m, st, y):
    with p.nc.Block() as block:
        @block.sync
        def _(eng):
            p.clear_last(eng, st)

        @block.scalar
        def _(eng):
            for k in range(CT):
                w, b = VEC["ln_w"][0] + k, VEC["ln_b"][0] + k
                eng.activation(y[:, k, :], y[:, k, :], ACT.Gelu, bias=m.vec[:, b:b + 1],
                               scale=m.vec[:, w:w + 1]).then_inc(st.gelu, 1)

        @block.vector
        def _(eng):
            for k in range(CT):
                eng.wait_ge(st.gelu, k + 1)
                eng.tensor_tensor(m.x[:, k, :], m.x[:, k, :], y[:, k, :], ALU.add).then_inc(st.added, 1)


def kron_raw(m):
    return m.big[:, 0:2, :].rearrange("p a n -> p (a n)")[0:3 * RANK, 0:FF]


def kron_weights(m, st, eng):
    raw, w_up = kron_raw(m), m.kron_up
    eng.wait_ge(st.raw, 16)
    eng.tensor_copy(w_up[0:3 * RANK, :], raw).then_inc(st.w_up, 1)
    eng.wait_ge(st.w_up, 1)
    eng.tensor_tensor(w_up[2 * RANK:3 * RANK, :], raw[2 * RANK:3 * RANK, :],
                      w_up[2 * RANK:3 * RANK, :].bitcast(F32), ALU.subtract).then_inc(st.w_up, 1)


def kron_ffn(p, m, st, u, w):
    nc, ps = p.nc, m.ps
    SLOTS = 4
    HRING = 4
    hid = m.prod[:, 0:2, :].rearrange("p a (b n) -> p (a b) n", n=HALF)
    z, g, h_hi, h_lo, w_up = m.kron_z, m.Bb[:, 1, :], m.kron_h_hi, m.kron_h_lo, m.kron_up
    with nc.Block() as block:
        @block.sync
        def _(eng):
            p.clear_last(eng, st)

        @block.gpsimd
        def _(eng):
            eng.wait_ge(st.loaded, 16)
            for k in range(CT):
                eng.tensor_copy(w.w_in_hi[:, k, :], w.raw[:, k, :]).then_inc(st.w_in, 1)
                eng.wait_ge(st.w_in, 2 * k + 1)
                eng.tensor_tensor(w.w_in_lo[:, k, :], w.raw[:, k, :], w.w_in_hi[:, k, :].bitcast(F32),
                                  ALU.subtract).then_inc(st.w_in, 1)
                eng.wait_ge(st.w_in, 2 * k + 2)

        @block.tensor
        def _(eng):
            for c in range(NH):
                for k in range(CT):
                    mm = eng.matmul(ps[0:3 * RANK, c, :], m.kin[:, k, :], u[:, k, cols(c)], start=k == 0, stop=k == CT - 1)
                mm.then_inc(st.narrow, 1)

            def up(s):
                c, f = s // FT, s % FT
                if s == 0:
                    eng.wait_ge(st.w_up, 2)
                if f == 0:
                    eng.wait_ge(st.z, 2 * (c + 1))
                if s >= SLOTS:
                    eng.wait_ge(st.gelu, s - SLOTS + 1)
                eng.matmul(ps[:, 2 + s % SLOTS, :], w_up[0:3 * RANK, f * P:(f + 1) * P],
                           z[0:3 * RANK, cols(c)], start=True, stop=True).then_inc(st.up, 1)

            def down(s):
                c, f = s // FT, s % FT
                eng.wait_ge(st.split, s + 1)
                eng.matmul(ps[0:2 * RANK, 6 + c, :], m.proj1[:, f, :], h_hi[:, s % HRING, :], start=f == 0, stop=False,
                           skip_group_check=True)
                eng.matmul(ps[0:2 * RANK, 6 + c, :], m.proj1[:, f, :], h_lo[:, s % HRING, :], start=False,
                           stop=f == FT - 1, skip_group_check=True).then_inc(st.down, 1)

            def widen(c):
                eng.wait_ge(st.g, c + 1)
                for k in range(CT):
                    s = c * CT + k
                    if s >= 2:
                        eng.wait_ge(st.added, s - 1)
                    eng.matmul(ps[:, s % 2, :], m.kout[0:2 * RANK, k * P:(k + 1) * P], g[0:2 * RANK, cols(c)],
                               start=True, stop=True).then_inc(st.wide, 1)

            up(0)
            up(1)
            for s in range(NH * FT):
                if s + 2 < NH * FT:
                    up(s + 2)
                down(s)
            for c in range(NH):
                widen(c)

        @block.scalar
        def _(eng):
            for s in range(NH * FT):
                eng.wait_ge(st.up, s + 1)
                if s >= HRING:
                    eng.wait_ge(st.split, s - HRING + 1)
                eng.activation(hid[:, s % HRING, :], ps[:, 2 + s % SLOTS, :], ACT.Gelu).then_inc(st.whole, 1)
                if s >= HRING:
                    eng.wait_ge(st.down, s - HRING + 1)
                eng.activation(h_hi[:, s % HRING, :], ps[:, 2 + s % SLOTS, :], ACT.Gelu).then_inc(st.gelu, 1)

        @block.vector
        def _(eng):
            for c in range(NH):
                eng.wait_ge(st.narrow, c + 1)
                eng.tensor_copy(z[0:3 * RANK, cols(c)], ps[0:3 * RANK, c, :]).then_inc(st.z, 1)
                eng.wait_ge(st.z, 2 * c + 1)
                eng.tensor_tensor(z[RANK:2 * RANK, cols(c)], ps[RANK:2 * RANK, c, :],
                                  z[RANK:2 * RANK, cols(c)].bitcast(F32), ALU.subtract).then_inc(st.z, 1)
            for s in range(NH * FT):
                eng.wait_ge(st.gelu, s + 1)
                eng.wait_ge(st.whole, s + 1)
                if s >= HRING:
                    eng.wait_ge(st.down, s - HRING + 1)
                eng.tensor_tensor(h_lo[:, s % HRING, :], hid[:, s % HRING, :], h_hi[:, s % HRING, :].bitcast(F32),
                                  ALU.subtract).then_inc(st.split, 1)
            for c in range(NH):
                eng.wait_ge(st.down, (c + 1) * FT)
                eng.tensor_copy(g[0:2 * RANK, cols(c)], ps[0:2 * RANK, 6 + c, :]).then_inc(st.g, 1)
            for c in range(NH):
                for k in range(CT):
                    s = c * CT + k
                    eng.wait_ge(st.wide, s + 1)
                    eng.tensor_tensor(m.x[:, k, cols(c)], m.x[:, k, cols(c)], ps[:, s % 2, :], ALU.add).then_inc(st.added, 1)


def in_projection(p, m, st, w, u, xin, z):
    nc, ps = p.nc, m.ps
    SETS = 4
    acc = m.prod
    with nc.Block() as block:
        @block.sync
        def _(eng):
            p.clear_last(eng, st)

        @block.tensor
        def _(eng):
            for f in range(2 * DT1):
                if f >= SETS:
                    t = (f - SETS) // 2
                    eng.wait_ge(st.silu_z if f % 2 else st.tap, t + 1 if f % 2 else TAPS * (t + 1))
                at = (f // 2) * P + (DI if f % 2 else 0)
                for c in range(NH):
                    if f == 0:
                        eng.wait_ge(st.split, c + 1)
                    for k in range(CT):
                        out_ap = ps[:, 2 * (f % SETS) + c, :]
                        w_hi, w_lo = w.w_in_hi[:, k, at:at + P], w.w_in_lo[:, k, at:at + P]
                        u_hi, u_lo = w.u_in_hi[:, k, cols(c)], w.u_in_lo[:, k, cols(c)]
                        eng.matmul(out_ap, w_hi, u_hi, start=k == 0, stop=False, skip_group_check=True)
                        eng.matmul(out_ap, w_hi, u_lo, start=False, stop=False, skip_group_check=True)
                        mm = eng.matmul(out_ap, w_lo, u_hi, start=False, stop=k == CT - 1, skip_group_check=True)
                mm.then_inc(st.product, 1)

        @block.vector
        def _(eng):
            for c in range(NH):
                eng.wait_ge(st.high, c + 1)
                eng.tensor_tensor(w.u_in_lo[:, :, cols(c)], u[:, :, cols(c)], w.u_in_hi[:, :, cols(c)].bitcast(F32),
                                  ALU.subtract).then_inc(st.split, 1)
            for t in range(DT1):
                f = 2 * t
                x = ps[:, 2 * (f % SETS):2 * (f % SETS) + 2, :].rearrange("p c n -> p (c n)")
                a = acc[:, t % 3, :]
                at, b = VEC["conv_w"][0] + t * TAPS, VEC["conv_b"][0] + t
                eng.wait_ge(st.product, f + 1)
                if t >= 3:
                    eng.wait_ge(st.silu_x, t - 2)
                eng.tensor_scalar(a, x, m.vec[:, at + TAPS - 1:at + TAPS], m.vec[:, b:b + 1], ALU.mult,
                                  ALU.add).then_inc(st.tap, 1)
                for s in range(1, TAPS):
                    eng.wait_ge(st.tap, TAPS * t + s)
                    i = eng.scalar_tensor_tensor(out=a[:, s:L], in0=x[:, 0:L - s], scalar=m.vec[:, at + TAPS - 1 - s:at + TAPS - s],
                                                 in1=a[:, s:L], op0=ALU.mult, op1=ALU.add)
                    i.then_inc(st.tap, 1)

        @block.scalar
        def _(eng):
            for c in range(NH):
                eng.activation(w.u_in_hi[:, :, cols(c)], u[:, :, cols(c)], ACT.Copy).then_inc(st.high, 1)
            for t in range(DT1):
                f = 2 * t + 1
                eng.wait_ge(st.product, f + 1)
                eng.activation(z[:, t, :].rearrange("p (c n) -> p c n", c=NH), ps[:, 2 * (f % SETS):2 * (f % SETS) + 2, :],
                               ACT.Silu).then_inc(st.silu_z, 1)
                eng.wait_ge(st.tap, TAPS * (t + 1))
                eng.activation(xin[:, t, :], acc[:, t % 3, :], ACT.Silu).then_inc(st.silu_x, 1)


def out_projection(p, m, st, w_out, y, z, out):
    nc, ps = p.nc, m.ps
    with nc.Block() as block:
        @block.sync
        def _(eng):
            p.clear_last(eng, st)

        @block.tensor
        def _(eng):
            for f in range(CT):
                for c in range(NH):
                    for k in range(DT1):
                        if f == 0 and c == 0:
                            eng.wait_ge(st.gated, k + 1)
                        mm = eng.matmul(ps[:, 2 * f + c, :], w_out[:, k, f * P:(f + 1) * P], z[:, k, cols(c)],
                                        start=k == 0, stop=k == DT1 - 1)
                mm.then_inc(st.product, 1)

        @block.vector
        def _(eng):
            for t in range(DT1):
                eng.tensor_tensor(z[:, t, :], z[:, t, :], y[:, t, :], ALU.mult).then_inc(st.gated, 1)

        @block.scalar
        def _(eng):
            for f in range(CT):
                eng.wait_ge(st.product, f + 1)
                eng.activation(out[:, f, :].rearrange("p (c n) -> p c n", c=NH), ps[:, 2 * f:2 * f + 2, :],
                               ACT.Copy).then_inc(st.copied, 1)


def affine_residual(p, m, st, y):
    with p.nc.Block() as block:
        @block.sync
        def _(eng):
            p.clear_last(eng, st)

        @block.vector
        def _(eng):
            for k in range(CT):
                g, b = VEC["gamma"][0] + k, VEC["beta"][0] + k
                eng.tensor_scalar(y[:, k, :], y[:, k, :], m.vec[:, g:g + 1], m.vec[:, b:b + 1], ALU.mult,
                                  ALU.add).then_inc(st.scaled, 1)
            for k in range(CT):
                eng.wait_ge(st.scaled, k + 1)
                eng.tensor_tensor(m.x[:, k, :], m.x[:, k, :], y[:, k, :], ALU.add).then_inc(st.added, 1)


def expert_slice(p, g, st, eng, i):
    e, s, slot = i // SLICES, i % SLICES, i % 2
    w = SLICE * P
    eng.dma_start(g.raw1[:, slot, :, :], p.io["w1"][:, e, :, s * w:(s + 1) * w]).then_inc(st.got[slot], 16)
    eng.dma_start(g.raw2[:, slot, :, :], p.io["w2"][:, e, s * SLICE:(s + 1) * SLICE, :]).then_inc(st.got[slot], 16)


def low_weights(g, st, eng, i):
    slot = i % 2
    eng.wait_ge(st.high, 2 * i + 2)
    eng.wait_ge(st.got[slot], 32 * (i // 2 + 1))
    for raw, hi, lo in ((g.raw1, g.w1_hi, g.w1_lo), (g.raw2, g.w2_hi, g.w2_lo)):
        if i >= 2:
            eng.wait_ge(st.down, (i - 1) * SLICE * NH)
        eng.tensor_tensor(lo[:, slot, :, :], raw[:, slot, :, :], hi[:, slot, :, :].bitcast(F32),
                          ALU.subtract).then_inc(st.split, 1)


def first_slice(g, st, eng):
    eng.memset(g.ones[:, :], 1.0).then_inc(st.ones, 1)
    eng.wait_ge(st.ones, 1)
    eng.wait_ge(st.got[0], 32)
    eng.tensor_copy(g.w1_hi[:, 0, :, :], g.raw1[:, 0, :, :]).then_inc(st.high, 1)
    eng.wait_ge(st.high, 1)
    eng.tensor_copy(g.w2_hi[:, 0, :, :], g.raw2[:, 0, :, :]).then_inc(st.high, 1)
    low_weights(g, st, eng, 0)


def gate_scores(m, g, st, eng, c):
    gw = m.vec[:, VEC["gate_w"][0]:VEC["gate_w"][1]].rearrange("p (k e) -> p k e", e=E)
    tiles = HALF // P
    for t in range(c * tiles, (c + 1) * tiles):
        for k in range(CT):
            mm = eng.matmul(m.ps[:, 6, t * E:(t + 1) * E], g.un[:, k, t * P:(t + 1) * P], gw[:, k, :],
                            start=k == 0, stop=k == CT - 1)
    mm.then_inc(st.scores, 1)


def experts(p, m, g, st, image, out, following):
    nc, ps = p.nc, m.ps
    UNITS = SLICE * NH
    ALL = E * SLICES * UNITS
    RING = 3
    FIRST_ROW = 12
    ROWS = E * NH
    LEAD = 1
    gb = m.vec[:, VEC["gate_b"][0]:VEC["gate_b"][1]]
    pr, rank, t1, t2 = g.probs, g.rank, g.t1, g.t2

    def passes(eng, out_ap, w_hi, w_lo, x_hi, x_lo, start, stop):
        eng.matmul(out_ap, w_hi, x_hi, start=start, stop=False, skip_group_check=True)
        eng.matmul(out_ap, w_hi, x_lo, start=False, stop=False, skip_group_check=True)
        return eng.matmul(out_ap, w_lo, x_hi, start=False, stop=stop, skip_group_check=True)

    with nc.Block() as block:
        @block.sync
        def _(eng):
            p.clear_last(eng, st)
            for i in range(2, E * SLICES):
                eng.wait_ge(st.split, 2 * (i - 1))
                expert_slice(p, g, st, eng, i)
            for c in range(NH):
                eng.wait_ge(st.added, (E - 1) * CT * NH + (c + 1) * CT)
                eng.dma_start(out[:, :, cols(c)], g.tmp[:, c * CT:(c + 1) * CT, :]).then_inc(image.stored, 16)
                load_half(eng, m, image, following, c)

        @block.gpsimd
        def _(eng):
            for i in range(1, E * SLICES):
                low_weights(g, st, eng, i)

        @block.scalar
        def _(eng):
            def gelu(i, v):
                e, s, u = i // SLICES, i % SLICES, i * UNITS + v
                t = s * SLICE + v // NH
                b = VEC["b1"][0] + e * HT + t
                eng.wait_ge(st.hidden, u + 1)
                if u >= RING:
                    eng.wait_ge(st.h_split, u - RING + 1)
                eng.activation(g.hid[:, u % RING, :], ps[:, 6 + u % 2, :], ACT.Gelu,
                               bias=m.vec[:, b:b + 1]).then_inc(st.gelu, 1)

            def high(i):
                slot = i % 2
                eng.wait_ge(st.got[slot], 32 * (i // 2 + 1))
                for raw, hi in ((g.raw1, g.w1_hi), (g.raw2, g.w2_hi)):
                    if i >= 2:
                        eng.wait_ge(st.down, (i - 1) * UNITS)
                        eng.wait_ge(st.split, 2 * (i - 1))
                    eng.activation(hi[:, slot, :, :], raw[:, slot, :, :], ACT.Copy).then_inc(st.high, 1)

            for c in range(NH):
                eng.activation(g.u_hi[:, :, cols(c)], g.un[:, :, cols(c)], ACT.Copy).then_inc(st.u_high, 1)
            for i in range(E * SLICES):
                for v in range(UNITS):
                    gelu(i, v)
                    if i == 0 and v == 1:
                        eng.wait_ge(st.step, 3)
                        eng.activation(pr[:, :, :], pr[:, :, :], ACT.Exp).then_inc(st.exped, 1)
                    if v == 1 and i < E * SLICES - 1:
                        high(i + 1)

        @block.vector
        def _(eng):
            n = [0]

            def then(ins):
                n[0] += 1
                ins.then_inc(st.step, 1)
                eng.wait_ge(st.step, n[0])

            def each(ap):
                return ap.unsqueeze(2).to_broadcast([P, TT, E])

            def shift_scores():
                eng.wait_ge(st.scores, NH)
                then(eng.tensor_tensor(pr[:, :, :], ps[:, 6, 0:TT * E].rearrange("p (t e) -> p t e", e=E),
                                       gb.unsqueeze(1).to_broadcast([P, TT, E]), ALU.add))
                then(eng.tensor_reduce(t1[:, :], pr[:, :, :], AX.X, ALU.max))
                then(eng.tensor_tensor(pr[:, :, :], pr[:, :, :], each(t1[:, :]), ALU.subtract))

            def norm_probs():
                eng.wait_ge(st.exped, 1)
                then(eng.tensor_reduce(t1[:, :], pr[:, :, :], AX.X, ALU.add))
                then(eng.reciprocal(t2[:, :], t1[:, :]))
                then(eng.tensor_tensor(pr[:, :, :], pr[:, :, :], each(t2[:, :]), ALU.mult))

            def rank_expert(e):
                first = True
                for o in range(E):
                    if o == e:
                        continue
                    dst = rank[:, :, e] if first else t1[:, :]
                    then(eng.tensor_tensor(dst, pr[:, :, o], pr[:, :, e], ALU.is_ge if o < e else ALU.is_gt))
                    if not first:
                        then(eng.tensor_tensor(rank[:, :, e], rank[:, :, e], t1[:, :], ALU.add))
                    first = False

            def keep_two():
                then(eng.tensor_scalar(rank[:, :, :], rank[:, :, :], 2.0, None, ALU.is_lt))
                then(eng.tensor_tensor(pr[:, :, :], pr[:, :, :], rank[:, :, :], ALU.mult))
                then(eng.tensor_reduce(t1[:, :], pr[:, :, :], AX.X, ALU.add))
                then(eng.tensor_scalar(t1[:, :], t1[:, :], 1e-9, None, ALU.add))
                then(eng.reciprocal(t2[:, :], t1[:, :]))
                then(eng.tensor_tensor(g.comb[:, :, :], pr[:, :, :], each(t2[:, :]), ALU.mult))

            def comb_diagonal(r):
                e, c = r // NH, r % NH
                if e:
                    eng.wait_ge(st.rows, r - NH + 1)
                for t in range(HALF // P):
                    tile = c * (HALF // P) + t
                    eng.tensor_scalar(g.diag[:, tile, :], m.ident[:, :], g.comb[:, tile, e:e + 1], None,
                                      ALU.mult).then_inc(st.diag, 1)

            def take_row(r):
                e, c = r // NH, r % NH
                eng.wait_ge(st.rows, r + 1)
                eng.tensor_copy(g.row[:, e, cols(c)], ps[:, 6 + c, :]).then_inc(st.row_taken, 1)

            def split_unit(u):
                eng.wait_ge(st.gelu, u + 1)
                if u >= RING:
                    eng.wait_ge(st.down, u - RING + 1)
                eng.tensor_copy(g.h_hi[:, u % RING, :], g.hid[:, u % RING, :]).then_inc(st.h_high, 1)
                eng.wait_ge(st.h_high, u + 1)
                eng.tensor_tensor(g.h_lo[:, u % RING, :], g.hid[:, u % RING, :],
                                  g.h_hi[:, u % RING, :].bitcast(F32), ALU.subtract).then_inc(st.h_split, 1)

            def weigh(e, c):
                eng.wait_ge(st.down, (e + 1) * SLICES * UNITS - (NH - 1 - c))
                for f in range(CT):
                    b = VEC["b2"][0] + e * CT + f
                    if e:
                        eng.wait_ge(st.added, (e - 1) * CT * NH + c * CT + f + 1)
                    eng.wait_ge(st.row_taken, ROWS)
                    eng.scalar_tensor_tensor(out=g.tmp[:, c * CT + f, :], in0=ps[:, 2 * f + c, :],
                                             scalar=m.vec[:, b:b + 1], in1=g.row[:, e, cols(c)], op0=ALU.add,
                                             op1=ALU.mult).then_inc(st.weighed, 1)

            def accumulate(e, c):
                for f in range(CT):
                    s = e * CT * NH + c * CT + f
                    eng.wait_ge(st.weighed, s + 1)
                    if e:
                        eng.wait_ge(st.added, s - CT * NH + 1)
                    dst = m.x[:, f, cols(c)] if e < E - 1 else g.tmp[:, c * CT + f, :]
                    eng.tensor_tensor(dst, m.x[:, f, cols(c)], g.tmp[:, c * CT + f, :], ALU.add).then_inc(st.added, 1)

            for c in range(NH):
                eng.wait_ge(st.u_high, c + 1)
                eng.tensor_tensor(g.u_lo[:, :, cols(c)], g.un[:, :, cols(c)], g.u_hi[:, :, cols(c)].bitcast(F32),
                                  ALU.subtract).then_inc(st.u_split, 1)
                if c == 0:
                    shift_scores()
            PER_EXPERT = SLICES * UNITS
            for u in range(ALL):
                split_unit(u)
                if u == 3:
                    norm_probs()
                if 4 <= u < 4 + E:
                    rank_expert(u - 4)
                if u == 8:
                    keep_two()
                if 0 <= u - FIRST_ROW - 1 < ROWS:
                    take_row(u - FIRST_ROW - 1)
                if 0 <= u - FIRST_ROW + LEAD < ROWS:
                    comb_diagonal(u - FIRST_ROW + LEAD)
                e, at = u // PER_EXPERT, u % PER_EXPERT
                if at == PER_EXPERT - 1:
                    weigh(e, 0)
                if e and at < NH:
                    if at == 0:
                        weigh(e - 1, 1)
                    accumulate(e - 1, at)
            accumulate(E - 1, 0)
            weigh(E - 1, 1)
            accumulate(E - 1, 1)

        @block.tensor
        def _(eng):
            def row_product(r):
                c = r % NH
                eng.wait_ge(st.diag, (r + 1) * (HALF // P))
                eng.wait_ge(st.gelu, FIRST_ROW + r + 1)
                for t in range(HALF // P):
                    mm = eng.matmul(ps[:, 6 + c, t * P:(t + 1) * P], g.ones[:, :], g.diag[:, c * (HALF // P) + t, :],
                                    start=True, stop=True)
                mm.then_inc(st.rows, 1)

            def up(i, v):
                slot, u = i % 2, i * UNITS + v
                t, c = v // NH, v % NH
                if v == 0:
                    eng.wait_ge(st.split, 2 * (i + 1))
                if u < NH:
                    eng.wait_ge(st.u_split, c + 1)
                if u == 0:
                    eng.wait_ge(st.step, 1)
                if u >= 2:
                    eng.wait_ge(st.gelu, u - 1)
                if 0 <= u - 2 - FIRST_ROW < ROWS:
                    eng.wait_ge(st.row_taken, u - 2 - FIRST_ROW + 1)
                for k in range(CT):
                    w = slice(t * P, (t + 1) * P)
                    mm = passes(eng, ps[:, 6 + u % 2, :], g.w1_hi[:, slot, k, w], g.w1_lo[:, slot, k, w],
                                g.u_hi[:, k, cols(c)], g.u_lo[:, k, cols(c)], k == 0, k == CT - 1)
                mm.then_inc(st.hidden, 1)

            def down(i, v):
                e, s, slot, u = i // SLICES, i % SLICES, i % 2, i * UNITS + v
                t, c = v // NH, v % NH
                if e and s == 0 and v < NH:
                    eng.wait_ge(st.weighed, (e - 1) * CT * NH + (v + 1) * CT)
                eng.wait_ge(st.h_split, u + 1)
                for f in range(CT):
                    w = slice(f * P, (f + 1) * P)
                    mm = passes(eng, ps[:, 2 * f + c, :], g.w2_hi[:, slot, t, w], g.w2_lo[:, slot, t, w],
                                g.h_hi[:, u % RING, :], g.h_lo[:, u % RING, :], s == 0 and t == 0,
                                s == SLICES - 1 and t == SLICE - 1)
                mm.then_inc(st.down, 1)

            gate_scores(m, g, st, eng, 1)
            up(0, 0)
            up(0, 1)
            for u in range(ALL):
                r = u - FIRST_ROW
                ahead = divmod(u + 2, UNITS) if u + 2 < ALL else None
                if 0 <= r < ROWS:
                    row_product(r)
                    down(*divmod(u, UNITS))
                    up(*ahead)
                else:
                    if ahead:
                        up(*ahead)
                    down(*divmod(u, UNITS))


def build(nc, io, out):
    with ExitStack() as ctx:
        p = Program(nc, io)
        banks = ctx.enter_context(nc.psum_tensor("banks", [P, 8, HALF], F32))
        resident = tensors(nc, ctx, [
                ("x", [P, CT, L], F32), ("vec", [P, VEC_N], F32), ("ident", [P, P], F32), ("mean_mat", [P, P], F32),
                ("pick", [P, BC], BF16), ("eps5", [P, 1], F32), ("eps6", [P, 1], F32), ("Dsum", [P, CT], F32),
                ("kin", [P, CT, 3 * RANK], F32), ("kout", [P, C], F32), ("A0", [P, K0 * N * CT], F32),
                ("A1", [P, N * DT1], F32), ("w0x", [P, K0, CT, 96 + R0], F32), ("lowk", [P, K0 * C + DI], F32),
                ("proj1", [P, FT, 2 * RANK], F32R), ("w1x", [P, DT1, 96 + R1], F32)])

        def stage(name, *signals):
            return semaphores(nc, ctx, name, *signals)

        s_load = stage("load", "small", "alog", "kron", "big", "split", "own", "exped")
        ln = ("mean", "centred", "squared", "variance", "logged", "rstd", "normed")
        s_image = stage("image", "stored", "loaded0", "loaded1")
        s_image.loaded = (s_image.loaded0, s_image.loaded1)
        s_norm = [stage("norm_a", *ln), stage("norm_b", *ln)]
        s_scan = stage("scan", "projected", "ones", "first", "low", "left", "second", "third", "parts", "dt", "capped",
                       "got_dt", "exped", "logged", "loaded", "turned", "delta", "du", "evacuated", "broadcast", "decay", "dbu", "scanned", "prod", "summed",
                       "taken")
        s_gelu = stage("gelu", "gelu", "added")
        s_ffn = stage("ffn", "loaded", "w_in", "raw", "w_up", "narrow", "z", "up", "whole", "gelu", "split", "down", "g", "wide", "added")
        s_xz = stage("xz", "high", "split", "product", "tap", "silu_z", "silu_x")
        s_out = stage("out", "gated", "product", "copied")
        s_aff = stage("affine", "scaled", "added")
        s_moe = stage("moe", "ones", "got0", "got1", "scores", "step", "exped", "u_high", "u_split", "high", "split", "hidden", "gelu", "h_high", "h_split", "down",
                      "diag", "rows", "row_taken", "weighed", "added")
        s_moe.got = [s_moe.got0, s_moe.got1]

        with ExitStack() as once:
            m = Named(ps=banks, **resident, **tensors(nc, once, [
                ("kmask", [P, CT, 3 * RANK], F32), ("emask", [P, C], F32), ("c2p", [P, C], F32),
                    ("fc2", [P, FT, RANK], F32)]))
            load_weights(p, m, s_load, s_image)
        with nc.Block() as block:
            @block.sync
            def _(eng):
                p.clear_last(eng, None)

        p.last = s_moe
        with nc.Fori(0, B) as b:
            with ExitStack() as conv:
                m = Named(ps=banks, **resident, **tensors(nc, conv, [
                        ("h", [P, CT, L], F32),
                        ("prod", [P, CT, L], F32),
                        ("Bb", [P, 2, L], F32), ("Cb", [P, 2, L], F32),
                        ("big", [P, 4 * CT, L], F32)]))

                def scan_tensors(stack, layer):
                    made = tensors(nc, stack, [
                        (f"delta{layer}", [P, 2, CT, L], F32), (f"du{layer}", [P, 2, CT, L], F32),
                        (f"dA{layer}", [P, CT, L], F32), (f"dBu{layer}", [P, CT, L], F32),
                        (f"parts{layer}", [P, 2, L], BF16), (f"low{layer}", [P, L], F32)])
                    return Named(m, **{name[:-1]: t for name, t in made.items()})

                rstd = m.Cb[:, 0, :]
                u, ut, ys = m.big[:, 0:CT, :], m.big[:, CT:2 * CT, :], m.big[:, 2 * CT:3 * CT, :]

                layer_norm(p, m, s_norm[0], m.x, u, m.prod, rstd, m.eps6, loaded=s_image.loaded,
                           fetch=lambda eng: eng.wait_ge(s_image.stored, 16 * NH))
                p.last = Named(all=s_norm[0].all + s_image.all)
                def take_first(eng, j, y):
                    eng.scalar_tensor_tensor(out=ys[:, j, :], in0=u[:, j, :], scalar=m.Dsum[:, j:j + 1], in1=y,
                                             op0=ALU.mult, op1=ALU.add).then_inc(s_scan.taken, 1)

                def take_more(eng, j, y):
                    eng.tensor_tensor(ys[:, j, :], ys[:, j, :], y, ALU.add).then_inc(s_scan.taken, 1)

                def take_turned(eng, j, y):
                    v = ys[:, j, :].rearrange("p (h w) -> p h w", w=WW)
                    eng.tensor_tensor(v, v, y.rearrange("p (w h) -> p h w", w=WW), ALU.add).then_inc(s_scan.taken, 1)

                def direction(k, take):
                    src = ut if k % 2 else u
                    return Named(project=True, kts=[src[:, t, :] for t in range(CT)], wx=lambda t: m.w0x[:, k, t, :],
                                 rank=R0, dt_at=k * C, u=lambda j: src[:, j, :],
                                 A=m.A0, a_at=k * N * CT, reverse=k >= 2, take=take, after=take is not take_first)

                with ExitStack() as scans:
                    selective_scans(p, scan_tensors(scans, 0), s_scan,
                                    [direction(0, take_first), direction(2, take_more),
                                     direction(1, take_turned), direction(3, take_turned)], turned=(u, ut))
                layer_norm(p, m, s_norm[0], ys, ys, m.prod, rstd, m.eps5)
                gated_residual(p, m, s_gelu, ys)

                w_raw = m.big[:, DT1:2 * DT1, :].rearrange("p a n -> p (a n)")[:, 0:CT * 2 * DI]
                w_raw = w_raw.rearrange("p (k n) -> p k n", k=CT)
                xin, z = m.big[:, 0:DT1, :], m.big[:, DT1:2 * DT1, :]
                with ExitStack() as wide:
                    w = Named(raw=w_raw, **tensors(nc, wide, [
                        ("w_in_hi", [P, CT, 2 * DI], F32R), ("w_in_lo", [P, CT, 2 * DI], F32R)]))
                    with ExitStack() as kron:
                        mk = Named(m, **tensors(nc, kron, [
                            ("kron_z", [P, L], F32R), ("kron_h_hi", [P, 4, HALF], F32R),
                            ("kron_h_lo", [P, 4, HALF], F32R), ("kron_up", [P, FF], F32R)]))

                        def fetch(eng):
                            eng.dma_start(kron_raw(m), io["fc1"]).then_inc(s_ffn.raw, 16)
                            eng.dma_start(w.raw, io["w_in"]).then_inc(s_ffn.loaded, 16)

                        layer_norm(p, m, s_norm[0], m.x, m.h, m.prod, rstd, m.eps5, fetch=fetch,
                                   aside=lambda eng: kron_weights(mk, s_ffn, eng))
                        kron_ffn(p, mk, s_ffn, m.h, w)

                    w = Named(w, **tensors(nc, wide, [("u_in_hi", [P, CT, L], F32R), ("u_in_lo", [P, CT, L], F32R)]))
                    layer_norm(p, m, s_norm[0], m.x, m.h, m.prod, rstd, m.eps6)
                    in_projection(p, m, s_xz, w, m.h, xin, z)
                scans = conv.enter_context(ExitStack())
                ms = scan_tensors(scans, 1)
                w_out = ms.delta[:, 0, :, :].rearrange("p k l -> p (k l)")[:, 0:DT1 * C]
                w_out = w_out.rearrange("p (k n) -> p k n", k=DT1)

                def group(t0):
                    def take_group(eng, j, y):
                        t, d = t0 + j, VEC["D1"][0] + t0 + j
                        eng.scalar_tensor_tensor(out=xin[:, t, :], in0=xin[:, t, :], scalar=m.vec[:, d:d + 1], in1=y,
                                                 op0=ALU.mult, op1=ALU.add).then_inc(s_scan.taken, 1)

                    return Named(project=t0 == 0, kts=[xin[:, t, :] for t in range(DT1)], wx=lambda t: m.w1x[:, t, :],
                                 rank=R1, dt_at=K0 * C + t0 * P, u=lambda j: xin[:, t0 + j, :],
                                 A=m.A1, a_at=t0 * N, reverse=False, take=take_group, after=False)

                selective_scans(p, ms, s_scan, [group(CT * i) for i in range(GROUPS1)],
                                load_ahead=lambda eng, done: eng.dma_start(w_out, p.io["w_out"]).then_inc(done, 16))
                out_projection(p, m, s_out, w_out, xin, z, m.h)
                layer_norm(p, m, s_norm[0], m.h, m.h, m.prod, rstd, m.eps5)
                affine_residual(p, m, s_aff, m.h)

            with ExitStack() as moe:
                SL = SLICE * P
                m = Named(ps=banks, **resident)
                g = Named(**tensors(nc, moe, [
                        ("un", [P, CT, L], F32),
                        ("u_hi", [P, CT, L], F32R), ("u_lo", [P, CT, L], F32R),
                        ("raw1", [P, 2, CT, SL], F32), ("raw2", [P, 2, SLICE, C], F32),
                        ("w1_hi", [P, 2, CT, SL], F32R), ("w1_lo", [P, 2, CT, SL], F32R),
                        ("w2_hi", [P, 2, SLICE, C], F32R), ("w2_lo", [P, 2, SLICE, C], F32R),
                        ("hid", [P, 3, HALF], F32), ("h_hi", [P, 3, HALF], F32R), ("h_lo", [P, 3, HALF], F32R),
                        ("row", [P, E, L], F32), ("tmp", [P, CT * NH, HALF], F32), ("diag", [P, TT, P], F32),
                        ("ones", [P, P], F32), ("probs", [P, TT, E], F32), ("rank", [P, TT, E], F32),
                        ("comb", [P, TT, E], F32), ("t1", [P, TT], F32), ("t2", [P, TT], F32)]))
                layer_norm(p, m, s_norm[1], m.x, g.un, g.tmp[:, :, :].rearrange("p (k c) n -> p k (c n)", c=NH), g.row[:, 0, :], m.eps5,
                           fetch=lambda eng: [expert_slice(p, g, s_moe, eng, i) for i in range(2)],
                           aside=lambda eng: first_slice(g, s_moe, eng),
                           after=lambda eng: gate_scores(m, g, s_moe, eng, 0))
                experts(p, m, g, s_moe, s_image, out[b], io["x"][b + 1])
        with nc.Block() as block:
            @block.sync
            def _(eng):
                eng.wait_ge(s_image.stored, 16 * NH)
                for loaded in s_image.loaded:
                    eng.wait_ge(loaded, 16)
                for s in s_image.all:
                    eng.sem_clear(s)
                p.clear_last(eng, None)


def kernel(**inputs):
    import concourse.bacc as bacc
    import ml_dtypes
    from concourse.bass_utils import run_bass_kernel_spmd

    a = {k: np.asarray(v) for k, v in inputs.items()}

    def rows(v, t):
        return v.reshape(t, P, *v.shape[1:]).swapaxes(0, 1)

    wx0 = a["L0_conv_x_proj_weight"]
    bc = wx0[:, R0:]
    wx0 = np.concatenate([bc, bc, bc, wx0[:, :R0]], axis=1).transpose(2, 0, 1)
    wx1 = a["L1_conv_x_proj_w"]
    bc = wx1[R1:]
    wx1 = np.concatenate([bc, bc, bc, wx1[:R1]], axis=0).T
    vec = {
        "D0": a["L0_conv_Ds"].reshape(K0 * CT, P).T,
        "D1": a["L1_conv_D"].reshape(DT1, P).T,
        "conv_w": rows(a["L1_conv_conv_w"], DT1).reshape(P, -1), "conv_b": a["L1_conv_conv_b"].reshape(DT1, P).T,
        "ln_w": a["L0_conv_ln_weight"].reshape(CT, P).T, "ln_b": a["L0_conv_ln_bias"].reshape(CT, P).T,
        "gamma": a["L1_conv_ln_gamma"].reshape(CT, P).T, "beta": a["L1_conv_ln_beta"].reshape(CT, P).T,
        "c2": np.tile(a["L0_ffn_c_fc_2"][0], RANK).reshape(CT, P).T,
        "gate_b": np.tile(a["L1_ffn_gate_b"][None], (P, 1)),
        "b1": a["L1_ffn_b1"].reshape(E * HT, P).T, "b2": a["L1_ffn_b2"].reshape(E * CT, P).T,
        "gate_w": rows(a["L1_ffn_gate_w"], CT).reshape(P, -1),
    }
    block = np.arange(C)[:, None] // KR == np.arange(RANK)[None]
    arrays = {
        "x": np.concatenate([a["x"], a["x"][:1]]).reshape(B + 1, CT, P, L).transpose(0, 2, 1, 3),
        "ident": np.eye(P, dtype=np.float32),
        "mean_mat": np.full((P, P), 1.0 / C, np.float32),
        "pick": (np.arange(P)[:, None] % BC == np.arange(BC)[None]).astype(ml_dtypes.bfloat16),
        "vec": np.concatenate([vec[n] for n in VEC], axis=1),
        "kmask": rows(np.tile(block.astype(np.float32), (1, 3)), CT),
        "emask": np.tile(block.T.astype(np.float32), (2, 1)),
        "c2p": np.tile(a["L0_ffn_c_proj_2"][:, 0], (2 * RANK, RANK)),
        "A0": a["L0_conv_A_logs"].reshape(K0, CT, P, N).transpose(2, 0, 3, 1).reshape(P, -1),
        "A1": a["L1_conv_A_log"].reshape(GROUPS1, CT, P, N).transpose(2, 0, 3, 1).reshape(P, -1),
        "w0x": wx0.reshape(CT, P, K0, 96 + R0).transpose(1, 2, 0, 3),
        "dtw0": np.concatenate([a["L0_conv_dt_projs_weight"].transpose(2, 0, 1).reshape(R0, K0 * C),
                                a["L0_conv_dt_projs_bias"].reshape(1, K0 * C)]),
        "dtw1": np.concatenate([a["L1_conv_dt_proj_w"].T, a["L1_conv_dt_proj_b"].reshape(1, DI)]),
        "fc1": np.tile(a["L0_ffn_c_fc_1"].T, (3, 1)),
        "proj1": rows(a["L0_ffn_c_proj_1"].T, FT),
        "w_in": rows(a["L1_conv_in_proj_w"].T, CT), "w1x": rows(wx1, DT1),
        "w_out": rows(a["L1_conv_out_proj_w"].T, DT1),
        "w1": a["L1_ffn_w1"].reshape(E, CT, P, HID).transpose(2, 0, 1, 3),
        "w2": a["L1_ffn_w2"].reshape(E, HT, P, C).transpose(2, 0, 1, 3),
    }
    arrays = {f"{n}_in": np.ascontiguousarray(v) for n, v in arrays.items()}
    nc = bacc.Bacc("TRN2", target_bir_lowering=False, num_devices=1)
    io = {n[:-3]: nc.dram_tensor(n, v.shape, mybir.dt.from_np(v.dtype), kind="ExternalInput").ap()
          for n, v in arrays.items()}
    out = nc.dram_tensor("out", (B, P, CT, L), F32, kind="ExternalOutput").ap()
    build(nc, io, out)
    r = run_bass_kernel_spmd(nc, [arrays], core_ids=[0])
    y = r.results[0]["out"]
    return y.transpose(0, 2, 1, 3).reshape(B, C, HH, WW)
```
